# Optimizing a Trainium2 kernel written in Bass

```python
import numpy as np
import jax
import jax.numpy as jnp

def _softmax(x, axis=-1):
    return jax.nn.softmax(x, axis=axis)

def _gelu(x):
    return jax.nn.gelu(x, approximate=True)

def _silu(x):
    return jax.nn.silu(x)

def _sigmoid(x):
    return jax.nn.sigmoid(x)

def _layernorm(x, axis=-1, eps=1e-05):
    m = jnp.mean(x, axis=axis, keepdims=True)
    v = jnp.var(x, axis=axis, keepdims=True)
    return (x - m) / jnp.sqrt(v + eps)

def _scatter_add(tgt, idx, src, axis=0):
    return tgt.at[idx].add(src)

def _segment_sum(src, seg, n):
    return jax.ops.segment_sum(src, seg, n)
kernel_name = 'mk_conv_seq_d2_conv_nhwc768_r2_0c302d'

def setup_inputs(seed: int=0):
    np.random.seed(seed)
    _w = jnp.asarray

    def _rec_inputs():
        import jax
        import jax.numpy as jnp
        _gk = jax.random.key(seed)
        x = -2.692e-05 + 0.9999 * jax.random.normal(jax.random.fold_in(_gk, 1), (4, 45, 90, 384), jnp.float32)
        return x
    x = _rec_inputs()

    def _L0_conv_setup():
        import jax, jax.numpy as jnp
        import numpy as np
        NUM_BLOCKS = 8
        BLOCK = 48
        FACTOR = 1
        LAM = 0.01
        FRAC = 1.0
        SCALE = 0.02

        def _softshrink(v, lam):
            return jnp.where(v > lam, v - lam, jnp.where(v < -lam, v + lam, 0.0))
        key = jax.random.key(seed)
        k1, k2, k3, k4, k5 = jax.random.split(key, 5)
        B, H, W, C = (4, 45, 90, 384)
        x = jax.random.normal(k1, (B, H, W, C), jnp.float32)
        w1 = SCALE * jax.random.normal(k2, (2, NUM_BLOCKS, BLOCK, BLOCK * FACTOR), jnp.float32)
        b1 = SCALE * jax.random.normal(k3, (2, NUM_BLOCKS, BLOCK * FACTOR), jnp.float32)
        w2 = SCALE * jax.random.normal(k4, (2, NUM_BLOCKS, BLOCK * FACTOR, BLOCK), jnp.float32)
        b2 = SCALE * jax.random.normal(k5, (2, NUM_BLOCKS, BLOCK), jnp.float32)
        return {'x': x, 'w1': w1, 'b1': b1, 'w2': w2, 'b2': b2}
    _L0_conv_all = _L0_conv_setup()
    _L0_conv_in = {k: v for k, v in _L0_conv_all.items() if k in ('w1', 'b1', 'w2', 'b2')}
    del _L0_conv_all

    def _L1_conv_setup():
        import jax, jax.numpy as jnp
        import numpy as np
        NUM_BLOCKS = 8
        SPARSITY = 0.01
        HARD_FRAC = 1.0
        HSF = 1
        SCALE = 0.02

        def _softshrink(v, lam):
            return jnp.sign(v) * jnp.maximum(jnp.abs(v) - lam, 0.0)
        key = jax.random.key(seed)
        ks = jax.random.split(key, 5)
        B, H, W, C = (4, 45, 90, 384)
        nb, bs = (NUM_BLOCKS, C // NUM_BLOCKS)
        x = jax.random.normal(ks[0], (B, H, W, C), jnp.float32)
        w1 = SCALE * jax.random.normal(ks[1], (2, nb, bs, bs * HSF), jnp.float32)
        b1 = SCALE * jax.random.normal(ks[2], (2, nb, bs * HSF), jnp.float32)
        w2 = SCALE * jax.random.normal(ks[3], (2, nb, bs * HSF, bs), jnp.float32)
        b2 = SCALE * jax.random.normal(ks[4], (2, nb, bs), jnp.float32)
        return {'x': x, 'w1': w1, 'b1': b1, 'w2': w2, 'b2': b2}
    _L1_conv_all = _L1_conv_setup()
    _L1_conv_in = {k: v for k, v in _L1_conv_all.items() if k in ('w1', 'b1', 'w2', 'b2')}
    del _L1_conv_all
    return {'x': x, 'L0_conv_w1': _L0_conv_in['w1'], 'L0_conv_b1': _L0_conv_in['b1'], 'L0_conv_w2': _L0_conv_in['w2'], 'L0_conv_b2': _L0_conv_in['b2'], 'L1_conv_w1': _L1_conv_in['w1'], 'L1_conv_b1': _L1_conv_in['b1'], 'L1_conv_w2': _L1_conv_in['w2'], 'L1_conv_b2': _L1_conv_in['b2']}

def reference(x, L0_conv_w1, L0_conv_b1, L0_conv_w2, L0_conv_b2, L1_conv_w1, L1_conv_b1, L1_conv_w2, L1_conv_b2):
    import jax
    import jax.numpy as jnp

    def _L0_conv_ref(x, w1, b1, w2, b2):
        import jax, jax.numpy as jnp
        import numpy as np
        NUM_BLOCKS = 8
        BLOCK = 48
        FACTOR = 1
        LAM = 0.01
        FRAC = 1.0
        SCALE = 0.02

        def _softshrink(v, lam):
            return jnp.where(v > lam, v - lam, jnp.where(v < -lam, v + lam, 0.0))
        B, H, W, C = x.shape
        xf = x.astype(jnp.float32)
        f = jnp.fft.fft2(xf, axes=(1, 2), norm='ortho')
        Xh = f.real - f.imag
        Wf = W // 2 + 1
        Xh = Xh[:, :, :Wf, :].reshape(B, H, Wf, NUM_BLOCKS, BLOCK)
        total = H // 2 + 1
        kept = int(total * FRAC)
        lo, hi = (total - kept, min(total + kept, H))
        Xk = Xh[:, lo:hi, :kept]
        o1 = jax.nn.relu(jnp.einsum('bhwni,nio->bhwno', Xk, w1[0]) + b1[0])
        o2 = jnp.einsum('bhwni,nio->bhwno', o1, w2[0]) + b2[0]
        spec = jnp.zeros((B, H, Wf, NUM_BLOCKS, BLOCK), jnp.float32)
        spec = spec.at[:, lo:hi, :kept].set(_softshrink(o2, LAM))
        spec = spec.reshape(B, H, Wf, C).astype(jnp.complex64)
        y = jnp.fft.ifft2(spec, s=(H, W), axes=(1, 2), norm='ortho').real
        return y.astype(x.dtype) + x

    def _L1_conv_ref(x, w1, b1, w2, b2):
        import jax, jax.numpy as jnp
        import numpy as np
        NUM_BLOCKS = 8
        SPARSITY = 0.01
        HARD_FRAC = 1.0
        HSF = 1
        SCALE = 0.02

        def _softshrink(v, lam):
            return jnp.sign(v) * jnp.maximum(jnp.abs(v) - lam, 0.0)
        bias = x
        B, H, W, C = x.shape
        nb, bs = (NUM_BLOCKS, C // NUM_BLOCKS)
        Wh = W // 2 + 1
        xf = jnp.fft.rfft2(x.astype(jnp.float32), axes=(1, 2), norm='ortho')
        xf = xf.reshape(B, H, Wh, nb, bs)
        total_modes = H // 2 + 1
        kept_modes = int(total_modes * HARD_FRAC)
        r0 = total_modes - kept_modes
        r1 = min(total_modes + kept_modes, H)
        c1 = min(kept_modes, Wh)
        xs = xf[:, r0:r1, :c1]
        xr, xi = (jnp.real(xs), jnp.imag(xs))
        mm = lambda a, w: jnp.einsum('bhwni,nio->bhwno', a, w)
        o1r = jax.nn.relu(mm(xr, w1[0]) - mm(xi, w1[1]) + b1[0])
        o1i = jax.nn.relu(mm(xi, w1[0]) + mm(xr, w1[1]) + b1[1])
        o2r = _softshrink(mm(o1r, w2[0]) - mm(o1i, w2[1]) + b2[0], SPARSITY)
        o2i = _softshrink(mm(o1i, w2[0]) + mm(o1r, w2[1]) + b2[1], SPARSITY)
        z = jnp.zeros((B, H, Wh, nb, bs), jnp.complex64)
        z = z.at[:, r0:r1, :c1].set((o2r + 1j * o2i).astype(jnp.complex64))
        y = jnp.fft.irfft2(z.reshape(B, H, Wh, C), s=(H, W), axes=(1, 2), norm='ortho')
        return y.astype(x.dtype) + bias

    def _gn(v, G=32, eps=1e-05):
        B_, H_, W_, C_ = v.shape
        g = v.reshape(B_, H_, W_, G, C_ // G)
        m = jnp.mean(g, axis=(1, 2, 4), keepdims=True)
        s = jnp.var(g, axis=(1, 2, 4), keepdims=True)
        return ((g - m) / jnp.sqrt(s + eps)).reshape(v.shape)

    def _ln_c(v, eps=1e-06):
        m = jnp.mean(v, axis=-1, keepdims=True)
        s = jnp.var(v, axis=-1, keepdims=True)
        return (v - m) / jnp.sqrt(s + eps)

    def _ln_t(v, eps=1e-05):
        m = jnp.mean(v, axis=-1, keepdims=True)
        s = jnp.var(v, axis=-1, keepdims=True)
        return (v - m) / jnp.sqrt(s + eps)

    def _to_tokens(v):
        B_, H_, W_, C_ = v.shape
        return v.reshape(B_, H_ * W_, C_)

    def _from_tokens(t, like):
        return t.reshape(like.shape)
    x = _L0_conv_ref(x, L0_conv_w1, L0_conv_b1, L0_conv_w2, L0_conv_b2)
    x = _L1_conv_ref(x, L1_conv_w1, L1_conv_b1, L1_conv_w2, L1_conv_b2)
    return x

_drawn_inputs = setup_inputs


def setup_inputs(seed=0):
    import zlib

    import numpy as np

    out = dict(_drawn_inputs(seed))
    spreads = {}
    factors = {'L0_conv_w1': 8.0,
     'L0_conv_b1': 8.0,
     'L0_conv_w2': 8.0,
     'L0_conv_b2': 8.0,
     'L1_conv_w1': 4.64,
     'L1_conv_b1': 8.0,
     'L1_conv_w2': 3.845,
     'L1_conv_b2': 3.753}
    for name, (base, spread) in spreads.items():
        noise = np.random.default_rng([zlib.crc32(name.encode()), seed]).standard_normal(out[name].shape)
        drawn = base * np.exp(spread * noise) if base else spread * noise
        out[name] = jnp.asarray(drawn.astype(out[name].dtype))
    for name, factor in factors.items():
        out[name] = (out[name] * factor).astype(out[name].dtype)
    return out
```

```python
from contextlib import ExitStack

import numpy as np

import concourse.bass as bass
from concourse import mybir

F32 = mybir.dt.float32
F32R = mybir.dt.float32r
ALU = mybir.AluOpType
ACT = mybir.ActivationFunctionType

B, H, W, C = 4, 45, 90, 384
KW = (H // 2 + 1)
KWP = KW + 1
BS = 48
NBLK = C // BS
LAM = 0.01
HH = H // 2 + 1
T2 = 64
PR = T2 + H
SUBS = 2
ITERS = B // SUBS
STEPK = 4
STEPS = KWP // STEPK
NM = STEPK * H
HP = (H + 1) // 2
FCH = 3
NFC = -(-HP // FCH)
XCH = 9
NXC = H // XCH
NCONST = {}


def constants():
    w, kw = np.arange(W), np.arange(KWP)
    h, kh = np.arange(H), np.arange(H)
    norm = 1 / np.sqrt(H * W)
    live = (kw < KW)
    parts = {}

    def put(name, rows):
        full = np.zeros((128, rows.shape[1]))
        full[: rows.shape[0]] = rows
        parts[name] = full

    aw = 2 * np.pi * np.outer(w, kw) / W
    put("w_fwd", np.concatenate([np.cos(aw) * live, np.sin(aw) * live], 1))
    ah = 2 * np.pi * np.outer(h, kh) / H
    co, si = np.cos(ah) * norm, np.sin(ah) * norm
    pair = lambda a, b: np.stack([a, b], 1).reshape(2 * H, H)
    put("h_cas", pair(co + si, co - si))
    put("h_re", pair(co, -si))
    put("h_im", pair(-si, -co))
    ci, sn = -np.cos(ah.T) * norm, -np.sin(ah.T) * norm
    real = np.concatenate([ci[:, :HH], sn[:, :HH]], 1)
    up = np.zeros((PR, 2 * HH))
    up[T2:] = real
    put("u0_lo", real)
    put("u0_hi", up)
    both = np.zeros((PR, 2 * H))
    both[:H] = np.concatenate([ci, sn], 1)
    both[T2:] = np.concatenate([-sn, ci], 1)
    put("u1", both)
    for name, weight, sign in (("w_pos", live * 1.0, -1), ("w_neg", live * 1.0, 1), ("w_one", live * np.where(kw == 0, 1.0, 2.0), -1)):
        rows = np.stack([np.cos(aw.T) * weight[:, None], sign * np.sin(aw.T) * weight[:, None]], 1).reshape(2 * KWP, W)
        put(name, np.concatenate([rows, rows], 0))
    put("ident", np.eye(128))
    sign = np.ones((128, 1))
    sign[BS:2 * BS] = -1
    put("sign", sign)
    at, where = 0, {}
    for name, a in parts.items():
        where[name] = (at, a.shape[1])
        at += a.shape[1]
    return np.concatenate(list(parts.values()), 1).astype(np.float32), where


def spectral_layers(nc, x, l0_w1, l0_b1, l0_w2, l0_b2, l1_w1, l1_b1, l1_w2, l1_b2, const, out, where):
    ctx = ExitStack()
    with ctx:
        sb = lambda name, shape, dt=F32: ctx.enter_context(nc.sbuf_tensor(name, shape, dt))
        sem = lambda name: ctx.enter_context(nc.semaphore(name))

        scr_f = [nc.dram_tensor(f"scr_f{s}", (H, 2 * KWP, C), F32, kind="Internal").ap() for s in range(SUBS)]
        scr_i = [[nc.dram_tensor(f"scr_i{l}{s}", (2, 2 * KWP, (HH, H)[l], C), F32, kind="Internal").ap()
                  for s in range(SUBS)] for l in range(2)]

        img = [sb(f"img{s}", [128, H, C]) for s in range(SUBS)]
        cst = sb("cst", [128, const.shape[1]])
        K = {n: cst[:, a:a + m] for n, (a, m) in where.items()}
        iw_hi = {n: sb(f"{n}_hi", [128, W], F32R) for n in ("w_pos", "w_neg", "w_one")}
        iw_lo = {n: sb(f"{n}_lo", [128, W], F32R) for n in ("w_pos", "w_neg", "w_one")}
        w1 = [sb("w1_0", [2 * BS + 1, NBLK // 2, 2 * BS]), sb("w1_1", [2 * BS + 1, NBLK, 2 * BS])]
        w2 = [sb("w2_0", [2 * BS + 1, NBLK // 2, 2 * BS]), sb("w2_1", [2 * BS + 1, NBLK, 2 * BS])]
        jring = sb("jring", [128, 6, C], F32R)
        grow = sb("grow", [128, STEPK, C])
        z = sb("z", [128, 2, 2 * C])
        xt = sb("xt", [2 * BS + 1, NBLK, NM])
        o1 = sb("o1", [2 * BS + 1, NBLK, NM])
        ss = sb("ss", [112, 4, STEPK * 2, T2])
        late = sb("late", [128, 4 * 2 * NM + STEPK * C])
        fring = late[:, 0:2 * FCH * C].rearrange("p (k j c) -> p k j c", k=2, j=FCH)
        clip = late[:, 0:4 * 2 * NM].rearrange("p (q n) -> p q n", q=4)
        spec = late[:, 4 * 2 * NM:].rearrange("p (k c) -> p k c", k=STEPK)
        et = sb("et", [128, 2, 2, C], F32R)
        ps = ctx.enter_context(nc.psum_tensor("ps", [128, 8, 512], F32))

        c_ld, w_ld, w_ok = sem("const_loaded"), sem("weights_loaded"), sem("weights_ready")
        img_clr = [sem(f"img{s}_cleared") for s in range(SUBS)]
        ps_clr, wfix = sem("psum_cleared"), sem("weights_cleared")
        x_ld = [[sem(f"x{s}_{k}_loaded") for k in range(NXC)] for s in range(SUBS)]
        y_st = [[sem(f"y{s}_{k}_stored") for k in range(NXC)] for s in range(SUBS)]
        fw_mm, fw_act, fw_dve = sem("fw_product"), sem("fw_copied_act"), sem("fw_copied_dve")
        f_st = [sem(f"f_slot{k}_stored") for k in range(2)]
        mid = []
        for l in range(2):
            m = {n: sem(f"l{l}_{n}") for n in ("a_mm", "b_mm", "c_mm", "d_mm", "t_mm", "e_mm", "a_act", "a_dve",
                                               "b_act", "b_dve", "c_act", "c_dve", "d_clip", "d_ss", "t_act", "t_dve",
                                               "e_hi", "e_lo", "g_ld")}
            m["e_st"] = [sem(f"l{l}_e_slot{k}_stored") for k in range(2)]
            mid.append(m)
        j_ld = [[sem(f"j{l}_slot{k}_loaded") for k in range((2, 3)[l])] for l in range(2)]
        iw_mm, iw_add = sem("iw_product"), sem("iw_added")

        JS, JH, JC = (2, 3), (3, 2), (-(-HH // 3), -(-H // 2))
        uses = lambda l, k: len(range(k, JC[l], JS[l]))
        jobs_of = lambda l, c: (min(3 * c + 3, HP) if l == 0 else c + 1)

        def phases():
            for l in range(2):
                for kind in ("fwd", "mid", "inv"):
                    for s in range(SUBS):
                        yield kind, l, s

        def fw_count(it, l, s):
            return (it * 2 + l) * SUBS + s

        def mid_count(it, s, i):
            return (it * SUBS + s) * STEPS + i

        def skewed(eng, first, rest, both):
            first(0)
            both(1, True)
            with eng.Fori(2, STEPS) as i:
                both(i, False)
            rest(STEPS - 1)

        def inv_rows(l, j):
            if l == 0:
                return [j, H - j] if j else [0]
            return [2 * j, 2 * j + 1][: H - 2 * j]

        def dve_copy(dst, src):
            return nc.vector.tensor_copy(dst, src)

        def dve_relu(dst, src):
            return nc.vector.tensor_scalar(dst, src, 0.0, None, ALU.max)

        def dve_mid(dve, l, s, it):
            m, nb = mid[l], (2, 4)[l]

            def d_ss(n):
                for q in range(nb):
                    dve.wait_ge(m["d_clip"], n * nb + q + 1)
                    rows = (2 * BS, T2 + BS)[l]
                    for r in range(2):
                        part = slice(r * NM, (r + 1) * NM)
                        dst = ss[0:rows, 2 * q + r, 0:STEPK, 0:H] if l == 0 else ss[0:rows, q, r:2 * STEPK:2, 0:H]
                        last = nc.vector.scalar_tensor_tensor(
                            out=dst, in0=clip[0:rows, q, part].rearrange("p (k m) -> p k m", m=H), scalar=2 * LAM,
                            in1=ps[0:rows, 4 + q, part].rearrange("p (k m) -> p k m", m=H), op0=ALU.min, op1=ALU.subtract)
                    last.then_inc(m["d_ss"], 1)

            def e_lo(n):
                for q in range(nb):
                    dve.wait_ge(m["e_hi"], n * nb + q + 1)
                    rows = (T2 + 2 * HH, 2 * H)[l]
                    nc.vector.tensor_tensor(et[0:rows, q % 2, 1, :], ps[0:rows, 4 + q, 0:C],
                                            et[0:rows, q % 2, 0, :].bitcast(F32), ALU.subtract).then_inc(m["e_lo"], 1)

            def first(i):
                n = mid_count(it, s, i)
                for q in range(1, nb, 2):
                    a_copy(dve, dve_copy, l, n, q, "a_dve")
                for q in range(1, nb, 2):
                    b_copy(dve, dve_copy, l, n, q, "b_dve")
                for q in range(1, nb, 2):
                    c_relu(dve, dve_relu, l, n, q, "c_dve")

            def rest(i):
                n = mid_count(it, s, i)
                d_ss(n)
                for q in range(1, nb, 2):
                    t_copy(dve, dve_copy, l, n, q, "t_dve")
                e_lo(n)

            def both(i, second):
                n, o = mid_count(it, s, i), mid_count(it, s, i - 1)
                for q in range(1, nb, 2):
                    a_copy(dve, dve_copy, l, n, q, "a_dve")
                d_ss(o)
                for q in range(1, nb, 2):
                    b_copy(dve, dve_copy, l, n, q, "b_dve")
                for q in range(1, nb, 2):
                    t_copy(dve, dve_copy, l, o, q, "t_dve")
                for q in range(1, nb, 2):
                    c_relu(dve, dve_relu, l, n, q, "c_dve")
                e_lo(o)

            skewed(dve, first, rest, both)

        def copy_fwd(eng, j, ph, l, s):
            c = j // FCH
            rows = T2 + 2 * KWP if 2 * j + 1 < H else 2 * KWP
            if c >= 2:
                eng.wait_ge(f_st[c % 2], 32 * (ph * (NFC // 2) + c // 2))
            elif (l, s) != (0, 0):
                eng.wait_ge(f_st[c % 2], 32 * (ph * (NFC // 2)))
            eng.wait_ge(fw_mm, ph * HP + j + 1)
            dst, src = fring[0:rows, c % 2, j % FCH, :], ps[0:rows, j % 8, 0:C]
            if j % 2 == 0:
                nc.scalar.activation(dst, src, ACT.Copy).then_inc(fw_act, 1)
            else:
                nc.vector.tensor_copy(dst, src).then_inc(fw_dve, 1)

        def a_copy(eng, copy, l, n, q, done):
            nb = (2, 4)[l]
            eng.wait_ge(mid[l]["a_mm"], n * nb + q + 1)
            if l == 0:
                dst, src = z[0:PR, q, 0:C], ps[0:PR, q, 0:C]
            else:
                dst = z[0:PR, q // 2, :].rearrange("p (b r c) -> p b r c", r=2, c=BS)[:, :, q % 2, :]
                src = ps[0:PR, q, 0:C].rearrange("p (b c) -> p b c", c=BS)
            copy(dst, src).then_inc(mid[l][done], 1)

        def b_copy(eng, copy, l, n, q, done):
            nb = (2, 4)[l]
            eng.wait_ge(mid[l]["b_mm"], n * nb + q + 1)
            pair, b0, bank = (q, 0, 2 + q) if l == 0 else (q // 2, 4 * (q % 2), q)
            dst = xt[0:2 * BS, b0:b0 + 4, pair * 2 * H:(pair + 1) * 2 * H].rearrange("p b (k m) -> p b k m", k=2)
            src = ps[0:2 * BS, bank, :].rearrange("p (b k m) -> p b k m", b=4, k=2)[:, :, :, 0:H]
            copy(dst, src).then_inc(mid[l][done], 1)

        def c_relu(eng, relu, l, n, q, done):
            nb = (2, 4)[l]
            eng.wait_ge(mid[l]["c_mm"], n * nb + q + 1)
            dst = o1[0:2 * BS, 2 * q:2 * q + 2, :].rearrange("p b n -> p (b n)")
            relu(dst, ps[0:2 * BS, q, 0:2 * NM]).then_inc(mid[l][done], 1)

        def t_copy(eng, copy, l, n, q, done):
            nb = (2, 4)[l]
            eng.wait_ge(mid[l]["t_mm"], n * nb + q + 1)
            if l == 0:
                dst, src = spec[0:PR, q, :], ps[0:PR, 6 + q, 0:C]
            else:
                dst = spec[0:PR, q, :].rearrange("p (b c) -> p b c", c=BS)
                src = ps[0:PR, 4 + q, :].rearrange("p (b c) -> p b c", c=T2)[:, :, 0:BS]
            copy(dst, src).then_inc(mid[l][done], 1)

        def act_copy(dst, src):
            return nc.scalar.activation(dst, src, ACT.Copy)

        def act_relu(dst, src):
            return nc.scalar.activation(dst, src, ACT.Relu)

        def act_mid(act, l, s, it):
            m, nb = mid[l], (2, 4)[l]
            ph_b = fw_count(it, l, SUBS - 1)

            def d_clip(n):
                for k in range(2):
                    act.wait_ge(f_st[k], (ph_b + 1) * 32 * NFC // 2)
                for q in range(nb):
                    act.wait_ge(m["d_mm"], n * nb + q + 1)
                    rows = (2 * BS, T2 + BS)[l]
                    act_relu(clip[0:rows, q, :], ps[0:rows, 4 + q, 0:2 * NM]).then_inc(m["d_clip"], 1)

            def e_hi(n, opens=False):
                for q in range(nb):
                    act.wait_ge(m["e_mm"], n * nb + q + 1)
                    if not (opens and q < 2):
                        act.wait_ge(m["e_st"][q % 2], 32 * n + 16 * (q // 2))
                    rows = (T2 + 2 * HH, 2 * H)[l]
                    act_copy(et[0:rows, q % 2, 0, :], ps[0:rows, 4 + q, 0:C]).then_inc(m["e_hi"], 1)

            def first(i):
                n = mid_count(it, s, i)
                for q in range(0, nb, 2):
                    a_copy(act, act_copy, l, n, q, "a_act")
                for q in range(0, nb, 2):
                    b_copy(act, act_copy, l, n, q, "b_act")
                for q in range(0, nb, 2):
                    c_relu(act, act_relu, l, n, q, "c_act")

            def rest(i):
                n = mid_count(it, s, i)
                d_clip(n)
                for q in range(0, nb, 2):
                    t_copy(act, act_copy, l, n, q, "t_act")
                e_hi(n)

            def both(i, second):
                n, o = mid_count(it, s, i), mid_count(it, s, i - 1)
                for q in range(0, nb, 2):
                    a_copy(act, act_copy, l, n, q, "a_act")
                d_clip(o)
                for q in range(0, nb, 2):
                    b_copy(act, act_copy, l, n, q, "b_act")
                for q in range(0, nb, 2):
                    t_copy(act, act_copy, l, o, q, "t_act")
                for q in range(0, nb, 2):
                    c_relu(act, act_relu, l, n, q, "c_act")
                e_hi(o, opens=second and s == 0)

            skewed(act, first, rest, both)

        block = ctx.enter_context(nc.Block())

        @block.sync
        def _(sp):
            def load_x(b, s, k):
                sp.dma_start(img[s][0:W, k * XCH:(k + 1) * XCH, :],
                             x[b, k * XCH:(k + 1) * XCH].rearrange("h w c -> w h c")).then_inc(x_ld[s][k], 16)

            for s in range(SUBS):
                for k in range(NXC):
                    sp.wait_ge(img_clr[s], k + 1)
                    load_x(s, s, k)
            for it in range(ITERS):
                for kind, l, s in phases():
                    if kind == "fwd":
                        ph = fw_count(it, l, s)
                        for c in range(NFC):
                            j0, j1 = c * FCH, min((c + 1) * FCH, HP)
                            sp.wait_ge(fw_act, ph * 12 + (j1 + 1) // 2)
                            sp.wait_ge(fw_dve, ph * 11 + j1 // 2)
                            for t in range(2):
                                n = len(range(2 * j0 + t, min(2 * j1, H), 2))
                                dst = scr_f[s][2 * j0 + t:2 * j0 + t + 2 * n - 1:2].rearrange("h q c -> q h c")
                                sp.dma_start(dst, fring[t * T2:t * T2 + 2 * KWP, c % 2, 0:n, :]).then_inc(f_st[c % 2], 16)
                    if kind == "mid":
                        m = mid[l]
                        for i in range(STEPS):
                            n = (it * SUBS + s) * STEPS + i
                            nb = (2, 4)[l]
                            for q in range(nb):
                                sp.wait_ge(m["e_lo"], n * nb + q + 1)
                                if l == 0:
                                    for t in range(2):
                                        kk = STEPK * i + 2 * q + t
                                        dst = scr_i[0][s][:, 2 * kk:2 * kk + 2].rearrange("e u h c -> (u h) e c")
                                        sp.dma_start(dst, et[t * T2:t * T2 + 2 * HH, q % 2, :, :].bitcast(F32)).then_inc(m["e_st"][q % 2], 16)
                                else:
                                    kk = STEPK * i + q
                                    dst = scr_i[1][s][:, 2 * kk:2 * kk + 2].rearrange("e u h c -> (u h) e c")
                                    sp.dma_start(dst, et[0:2 * H, q % 2, :, :].bitcast(F32)).then_inc(m["e_st"][q % 2], 16)
                    if kind == "inv" and l == 1:
                        ph = fw_count(it, l, s)
                        for k in range(NXC + 1):
                            if k < NXC:
                                sp.wait_ge(iw_add, ph * HP + min(-(-(k + 1) * XCH // 2), HP))
                                sp.dma_start(out[it * SUBS + s, k * XCH:(k + 1) * XCH].rearrange("h w c -> w h c"),
                                             img[s][0:W, k * XCH:(k + 1) * XCH, :]).then_inc(y_st[s][k], 16)
                            if k > 0 and it + 1 < ITERS:
                                sp.wait_ge(y_st[s][k - 1], 16 * (it + 1))
                                load_x((it + 1) * SUBS + s, s, k - 1)
            for s in range(SUBS):
                for k in range(NXC):
                    sp.wait_ge(y_st[s][k], 16 * ITERS)


        @block.gpsimd
        def _(pool):
            clears = [(t[:, :, :], 0.0) for t in (w1[0], w1[1], w2[0], w2[1])]
            clears += [(grow[T2:128, :, :], 0.0), (jring[2 * BS:128, :, :].bitcast(F32), 0.0), (ss[:, :, :, :], 0.0),
                       (xt[2 * BS:2 * BS + 1, :, :], 1.0), (o1[2 * BS:2 * BS + 1, :, :], 1.0)]
            for n, (t, v) in enumerate(clears):
                nc.gpsimd.memset(t, v).then_inc(wfix, 1)
                pool.wait_ge(wfix, n + 1)
            for k in range(NXC):
                nc.gpsimd.memset(img[1][T2:128, k * XCH:(k + 1) * XCH, :], 0.0).then_inc(img_clr[1], 1)
                pool.wait_ge(img_clr[1], k + 1)
            for it in range(ITERS):
                for kind, l, s in phases():
                    ph = fw_count(it, l, s)
                    if kind == "mid":
                        m, nb = mid[l], (2, 4)[l]
                        for k in range(2):
                            pool.wait_ge(f_st[k], (ph + 1) * 32 * NFC // 2)
                        rows = scr_f[s].rearrange("h (e k) c -> (h e) k c", e=2)
                        for i in range(STEPS):
                            pool.wait_ge(m["a_mm"], mid_count(it, s, i) * nb)
                            pool.dma_start(grow[0:2 * H, :, :], rows[:, i * STEPK:(i + 1) * STEPK, :]).then_inc(m["g_ld"], 16)
                    if kind == "inv":
                        for k in range(2):
                            pool.wait_ge(mid[l]["e_st"][k], (mid_count(it, s, 0) + STEPS) * (32, 32)[l])
                        rows = scr_i[l][s].rearrange("e q h c -> (e q) h c")
                        for c in range(JC[l]):
                            h0, h1 = c * JH[l], min((c + 1) * JH[l], (HH, H)[l])
                            if c < JS[l]:
                                pool.wait_ge(iw_mm, ph * HP)
                            else:
                                pool.wait_ge(iw_mm, ph * HP + jobs_of(l, c - JS[l]))
                            k = c % JS[l]
                            pool.dma_start(jring[0:4 * KWP, k * JH[l]:k * JH[l] + h1 - h0, :].bitcast(F32),
                                           rows[:, h0:h1, :]).then_inc(j_ld[l][k], 16)

        @block.scalar
        def _(act):
            act.dma_start(cst[:, :], const).then_inc(c_ld, 16)
            act.wait_ge(wfix, 4)
            n = 2 * BS
            for t, a, b in ((w1[0], l0_w1, l0_b1), (w2[0], l0_w2, l0_b2)):
                for j in range(2):
                    act.dma_start(t[j * BS:(j + 1) * BS, :, j * BS:(j + 1) * BS],
                                  a[0, j::2].rearrange("n i o -> i n o")).then_inc(w_ld, 16)
                act.dma_start(t[n:n + 1, :, :], b[0:1].rearrange("a (q j) o -> a q (j o)", j=2)).then_inc(w_ld, 16)
            for t, a, b in ((w1[1], l1_w1, l1_b1), (w2[1], l1_w2, l1_b2)):
                for i in range(2):
                    for o in range(2):
                        act.dma_start(t[i * BS:(i + 1) * BS, :, o * BS:(o + 1) * BS],
                                      a[i ^ o].rearrange("n i o -> i n o")).then_inc(w_ld, 16)
                for o in range(2):
                    act.dma_start(t[n:n + 1, :, o * BS:(o + 1) * BS], b[o:o + 1]).then_inc(w_ld, 16)
            act.wait_ge(ps_clr, 1)
            with act.Fori(0, ITERS) as it:
                for kind, l, s in phases():
                    ph = fw_count(it, l, s)
                    if kind == "fwd":
                        for j in range(0, HP, 2):
                            copy_fwd(act, j, ph, l, s)
                    if kind == "mid":
                        act_mid(act, l, s, it)

        @block.vector
        def _(dve):
            nc.vector.memset(ps[:, :, :], 0.0).then_inc(ps_clr, 1)
            for k in range(NXC):
                nc.vector.memset(img[0][T2:128, k * XCH:(k + 1) * XCH, :], 0.0).then_inc(img_clr[0], 1)
            dve.wait_ge(c_ld, 16)
            for n in iw_hi:
                nc.vector.tensor_copy(iw_hi[n][:, :], K[n]).then_inc(w_ok, 1)
            dve.wait_ge(w_ld, 16 * 18)
            dve.wait_ge(w_ok, 3)
            for n in iw_hi:
                nc.vector.tensor_tensor(iw_lo[n][:, :], K[n], iw_hi[n][:, :].bitcast(F32), ALU.subtract).then_inc(w_ok, 1)
            for t in (w1[1], w2[1]):
                v = t[0:2 * BS, :, 0:BS]
                nc.vector.tensor_scalar(v, v, K["sign"][0:2 * BS, :], None, ALU.mult).then_inc(w_ok, 1)
            for t in w2:
                v = t[2 * BS:2 * BS + 1, :, :]
                nc.vector.tensor_scalar(v, v, LAM, None, ALU.add).then_inc(w_ok, 1)
            with dve.Fori(0, ITERS) as it:
                for kind, l, s in phases():
                    ph = fw_count(it, l, s)
                    if kind == "fwd":
                        for j in range(1, HP, 2):
                            copy_fwd(dve, j, ph, l, s)
                    if kind == "mid":
                        dve_mid(dve, l, s, it)
                    if kind == "inv":
                        for j in range(HP):
                            dve.wait_ge(iw_mm, ph * HP + j + 1)
                            hs = inv_rows(l, j)
                            bank = 2 * (j % 4)
                            if len(hs) == 1:
                                y, p = img[s][0:W, hs[0], :], ps[0:W, bank, 0:C]
                            else:
                                y, p = img[s][0:W, hs[0]:hs[1] + 1:hs[1] - hs[0], :], ps[0:W, bank:bank + 2, 0:C]
                            nc.vector.tensor_tensor(y, p, y, ALU.add).then_inc(iw_add, 1)

        @block.tensor
        def _(pe):
            mm = nc.tensor.matmul
            pe.wait_ge(c_ld, 16)
            pe.wait_ge(ps_clr, 1)
            pe.wait_ge(wfix, 9)

            def fwd(l, s, it):
                ph = fw_count(it, l, s)
                for j in range(HP):
                    for k in range(NXC):
                        if l == 0 and 2 * j <= k * XCH < 2 * j + 2:
                            pe.wait_ge(x_ld[s][k], 16 * (it + 1))
                    if j >= 8:
                        if j % 2 == 0:
                            pe.wait_ge(fw_act, ph * 12 + (j - 8) // 2 + 1)
                        else:
                            pe.wait_ge(fw_dve, ph * 11 + (j - 8) // 2 + 1)
                    for t in range(2):
                        h = 2 * j + t
                        if h < H:
                            last = mm(ps[t * T2:t * T2 + 2 * KWP, j % 8, 0:C], K["w_fwd"], img[s][:, h, :], start=True, stop=True)
                    last.then_inc(fw_mm, 1)

            def inv(l, s, it):
                ph = fw_count(it, l, s)
                if (l, s) == (0, 0):
                    pe.wait_ge(w_ok, 10)
                for j in range(HP):
                    c, at = (j // 3, j % 3) if l == 0 else (j, 0)
                    k = c % JS[l]
                    if at == 0:
                        before = it * SUBS + s
                        pe.wait_ge(j_ld[l][k], 16 * (before * uses(l, k) + c // JS[l] + 1))
                    if j >= 4:
                        pe.wait_ge(iw_add, ph * HP + j - 3)
                    elif s == 1:
                        pe.wait_ge(iw_add, ph * HP + min(j - 2, 0))
                    for t, _h in enumerate(inv_rows(l, j)):
                        n = ("w_pos", "w_neg")[t] if l == 0 else "w_one"
                        row = jring[:, k * JH[l] + (at if l == 0 else t), :]
                        mm(ps[0:W, 2 * (j % 4) + t, 0:C], iw_hi[n][:, :], row, start=True, stop=False)
                        last = mm(ps[0:W, 2 * (j % 4) + t, 0:C], iw_lo[n][:, :], row, start=False, stop=True)
                    last.then_inc(iw_mm, 1)

            def middle(l, s, it):
                m, nb = mid[l], (2, 4)[l]
                half = nb // 2

                def a_h(n, opens=False):
                    pe.wait_ge(m["g_ld"], 16 * (n + 1))
                    if not opens:
                        pe.wait_ge(m["c_act"], n * half)
                        pe.wait_ge(m["c_dve"], n * half)
                    for q in range(nb):
                        pair, name = (q, "h_cas") if l == 0 else (q // 2, ("h_re", "h_im")[q % 2])
                        for t in range(2):
                            last = mm(ps[t * T2:t * T2 + H, q, 0:C], K[name], grow[:, 2 * pair + t, :], start=True, stop=True)
                        last.then_inc(m["a_mm"], 1)

                def b_transpose(n):
                    for q in range(nb):
                        pair, b0, bank = (q, 0, 2 + q) if l == 0 else (q // 2, 4 * (q % 2), q)
                        if l == 0:
                            pe.wait_ge(m[("a_act", "a_dve")[q]], n + 1)
                        elif q % 2 == 0:
                            pe.wait_ge(m["a_act"], n * 2 + pair + 1)
                            pe.wait_ge(m["a_dve"], n * 2 + pair + 1)
                        for b in range(4):
                            last = nc.tensor.transpose(ps[0:2 * BS, bank, b * 128:b * 128 + PR],
                                                       z[0:PR, pair, (b0 + b) * 2 * BS:(b0 + b + 1) * 2 * BS], K["ident"][0:PR, 0:PR])
                        last.then_inc(m["b_mm"], 1)

                def c_block(n):
                    pe.wait_ge(m["b_act"], (n + 1) * half)
                    pe.wait_ge(m["b_dve"], (n + 1) * half)
                    for q in range(nb):
                        for b in range(2):
                            last = mm(ps[0:2 * BS, q, b * NM:(b + 1) * NM], w1[l][:, 2 * q + b, :], xt[:, 2 * q + b, :], start=True, stop=True)
                        last.then_inc(m["c_mm"], 1)

                def d_block(n, opens=False):
                    pe.wait_ge(m["c_act"], (n + 1) * half)
                    pe.wait_ge(m["c_dve"], (n + 1) * half)
                    if not opens:
                        pe.wait_ge(m["e_lo"], n * nb)
                    for q in range(nb):
                        for r in range(2):
                            if l == 0:
                                last = mm(ps[0:2 * BS, 4 + q, r * NM:(r + 1) * NM], w2[0][:, 2 * q + r, :], o1[:, 2 * q + r, :], start=True, stop=True)
                            else:
                                for t in range(2):
                                    last = mm(ps[t * T2:t * T2 + BS, 4 + q, r * NM:(r + 1) * NM],
                                              w2[1][:, 2 * q + t, r * BS:(r + 1) * BS], o1[:, 2 * q + t, :], start=True, stop=True)
                        last.then_inc(m["d_mm"], 1)

                def t_transpose(n):
                    pe.wait_ge(m["d_ss"], (n + 1) * nb)
                    for q in range(nb):
                        rows, wide, bank = (2 * BS, 2 * BS, 6 + q) if l == 0 else (T2 + BS, 128, 4 + q)
                        for b in range(4):
                            modes = ss[0:rows, b, 2 * q:2 * q + 2, :].rearrange("p k m -> p (k m)")[:, 0:PR]
                            last = nc.tensor.transpose(ps[0:PR, bank, b * wide:b * wide + rows], modes, K["ident"][0:rows, 0:rows])
                        last.then_inc(m["t_mm"], 1)

                def e_h(n):
                    for q in range(nb):
                        eng = ("t_act", "t_dve")[q % 2]
                        pe.wait_ge(m[eng], n * half + q // 2 + 1)
                        if l == 0:
                            for t in range(2):
                                last = mm(ps[t * T2:t * T2 + 2 * HH, 4 + q, 0:C], K[("u0_lo", "u0_hi")[t]][0:PR, :],
                                          spec[0:PR, q, :], start=True, stop=True)
                        else:
                            last = mm(ps[0:2 * H, 4 + q, 0:C], K["u1"][0:PR, :], spec[0:PR, q, :], start=True, stop=True)
                        last.then_inc(m["e_mm"], 1)

                def first(i):
                    n = mid_count(it, s, i)
                    a_h(n, opens=s == 0)
                    b_transpose(n)
                    c_block(n)

                def rest(i):
                    n = mid_count(it, s, i)
                    d_block(n)
                    t_transpose(n)
                    e_h(n)

                def both(i, second):
                    n, o = mid_count(it, s, i), mid_count(it, s, i - 1)
                    a_h(n)
                    d_block(o, opens=second and s == 0)
                    b_transpose(n)
                    t_transpose(o)
                    c_block(n)
                    e_h(o)

                skewed(pe, first, rest, both)

            with pe.Fori(0, ITERS) as it:
                for kind, l, s in phases():
                    ph = fw_count(it, l, s)
                    if kind == "fwd":
                        if s == 1:
                            pe.wait_ge(fw_act, ph * 12)
                            pe.wait_ge(fw_dve, ph * 11)
                        fwd(l, s, it)
                    if kind == "mid":
                        if s == 0:
                            pe.wait_ge(fw_act, (ph + 2) * 12)
                            pe.wait_ge(fw_dve, (ph + 2) * 11)
                        if l == 0 and s == 0:
                            pe.wait_ge(w_ok, 10)
                        middle(l, s, it)
                    if kind == "inv":
                        if s == 0:
                            pe.wait_ge(mid[l]["e_lo"], (it * SUBS + SUBS) * STEPS * (2, 4)[l])
                        inv(l, s, it)
                        if s == SUBS - 1:
                            pe.wait_ge(iw_add, (ph + 1) * HP)
    return nc


def kernel(**inputs):
    import concourse.bacc as bacc
    from concourse.bass_utils import run_bass_kernel_spmd

    nc = bacc.Bacc("TRN2", target_bir_lowering=False, num_devices=1)
    const, where = constants()
    arrays, args = {}, []
    names = ["x"] + [f"L{l}_conv_{n}" for l in range(2) for n in ("w1", "b1", "w2", "b2")]
    for name in names:
        arrays[name] = np.ascontiguousarray(inputs[name])
    arrays["const"] = const
    for name, a in arrays.items():
        args.append(nc.dram_tensor(name, a.shape, mybir.dt.from_np(a.dtype), kind="ExternalInput").ap())
    out = nc.dram_tensor("y", (B, H, W, C), F32, kind="ExternalOutput").ap()
    spectral_layers(nc, *args, out, where)
    r = run_bass_kernel_spmd(nc, [arrays], core_ids=[0])
    return r.results[0]["y"]
```

```python
from contextlib import ExitStack

import numpy as np

import concourse.bass as bass
from concourse import mybir

F32 = mybir.dt.float32
F32R = mybir.dt.float32r
ALU = mybir.AluOpType
ACT = mybir.ActivationFunctionType

B, H, W, C = 4, 45, 90, 384
KW = (H // 2 + 1)
KWP = KW + 1
BS = 48
NBLK = C // BS
LAM = 0.01
HH = H // 2 + 1
T2 = 64
PR = T2 + H
SUBS = 2
ITERS = B // SUBS
STEPK = 4
STEPS = KWP // STEPK
NM = STEPK * H
HP = (H + 1) // 2
FCH = 2
NFC = -(-HP // FCH)
XCH = 9
NXC = H // XCH


def constants():
    w, kw = np.arange(W), np.arange(KWP)
    h, kh = np.arange(H), np.arange(H)
    norm = 1 / np.sqrt(H * W)
    live = (kw < KW)
    parts = {}

    def put(name, rows):
        full = np.zeros((128, rows.shape[1]))
        full[: rows.shape[0]] = rows
        parts[name] = full

    aw = 2 * np.pi * np.outer(w, kw) / W
    put("w_fwd", np.concatenate([np.cos(aw) * live, np.sin(aw) * live], 1))
    ah = 2 * np.pi * np.outer(h, kh) / H
    co, si = np.cos(ah) * norm, np.sin(ah) * norm
    pair = lambda a, b: np.stack([a, b], 1).reshape(2 * H, H)
    put("h_cas", pair(co + si, co - si))
    put("h_re", pair(co, -si))
    put("h_im", pair(-si, -co))
    ci, sn = -np.cos(ah.T) * norm, -np.sin(ah.T) * norm
    real = np.concatenate([ci[:, :HH], sn[:, :HH]], 1)
    up = np.zeros((PR, 2 * HH))
    up[T2:] = real
    put("u0_lo", real)
    put("u0_hi", up)
    both = np.zeros((PR, 2 * H))
    both[:H] = np.concatenate([ci, sn], 1)
    both[T2:] = np.concatenate([-sn, ci], 1)
    put("u1", both)
    for name, weight, sign in (("w_pos", live * 1.0, -1), ("w_neg", live * 1.0, 1), ("w_one", live * np.where(kw == 0, 1.0, 2.0), -1)):
        rows = np.stack([np.cos(aw.T) * weight[:, None], sign * np.sin(aw.T) * weight[:, None]], 1).reshape(2 * KWP, W)
        put(name, np.concatenate([rows, rows], 0))
    put("ident", np.eye(128))
    sign = np.ones((128, 1))
    sign[BS:2 * BS] = -1
    put("sign", sign)
    at, where = 0, {}
    for name, a in parts.items():
        where[name] = (at, a.shape[1])
        at += a.shape[1]
    return np.concatenate(list(parts.values()), 1).astype(np.float32), where


class Ring:

    def __init__(self, slots, uses):
        self.uses, self.total, self.count = uses, [0] * slots, {}
        for phase, (n, adds) in uses.items():
            for c, add in enumerate(adds):
                self.total[c % n] += add
                self.count[phase, c] = self.total[c % n]

    def slot(self, phase, c):
        return c % self.uses[phase][0]

    def landed(self, it, phase, c):
        return it * self.total[self.slot(phase, c)] + self.count[phase, c]

    def vacant(self, it, phase, c):
        before = self.count[phase, c] - self.uses[phase][1][c]
        return it * self.total[self.slot(phase, c)] + before if before else None

    def ended(self, it, phase):
        n, adds = self.uses[phase]
        last = {c % n: c for c in range(len(adds))}
        return [(k, self.landed(it, phase, c)) for k, c in last.items()]


def schedule():
    order = []

    def groups(kind, l, s):
        n = 4 if kind == "fwd" else 2
        return [(kind, l, s, tuple(range(j, min(j + n, HP)))) for j in range(0, HP, n)]

    def plain(gs):
        for g in gs:
            half[0] ^= 1
            order.append(g + (half[0],))

    half = [1]

    def middle(l, s, light, start, late=(), g0=None, j0=None):
        light = list(light)

        def gap(i, h):
            if i >= start and light:
                order.append(light.pop(0) + (h,))

        for i in range(STEPS):
            order.append(("a", l, s, i))
            if i == 0 and j0:
                order.append(("j0",) + j0)
            gap(i, 1)
            order.append(("b", l, s, i))
            if i:
                order.append(("d", l, s, i - 1))
            order.append(("c", l, s, i))
            if i:
                order.append(("t", l, s, i - 1))
            gap(i, 0)
            if i:
                order.append(("e", l, s, i - 1))
        half[0] = 0
        plain(light + list(late))
        if g0:
            order.append(("g0",) + g0)
        order.extend((k, l, s, STEPS - 1) for k in "dte")

    plain(groups("fwd", 0, 0))
    order.append(("g0", 0, 0))
    middle(0, 0, groups("fwd", 0, 1), 0, g0=(0, 1))
    middle(0, 1, groups("inv", 0, 0), 1, groups("fwd", 1, 0), g0=(1, 0), j0=(0, 0))
    middle(1, 0, groups("inv", 0, 1), 1, groups("fwd", 1, 1), g0=(1, 1), j0=(0, 1))
    middle(1, 1, groups("inv", 1, 0), 1, j0=(1, 0))
    order.append(("j0", 1, 1))
    plain(groups("inv", 1, 1))
    return order


def spectral_layers(nc, x, l0_w1, l0_b1, l0_w2, l0_b2, l1_w1, l1_b1, l1_w2, l1_b2, const, out, where):
    ctx = ExitStack()
    with ctx:
        sb = lambda name, shape, dt=F32: ctx.enter_context(nc.sbuf_tensor(name, shape, dt))
        sem = lambda name: ctx.enter_context(nc.semaphore(name))

        scr_f = [nc.dram_tensor(f"scr_f{s}", (H, 2 * KWP, C), F32, kind="Internal").ap() for s in range(SUBS)]
        scr_i = [[nc.dram_tensor(f"scr_i{l}{s}", (2, 2 * KWP, (HH, H)[l], C), F32, kind="Internal").ap()
                  for s in range(SUBS)] for l in range(2)]

        img = [sb(f"img{s}", [128, H, C]) for s in range(SUBS)]
        cst = sb("cst", [128, const.shape[1]])
        K = {n: cst[:, a:a + m] for n, (a, m) in where.items()}
        iw_hi = {n: sb(f"{n}_hi", [128, W], F32R) for n in ("w_pos", "w_neg", "w_one")}
        iw_lo = {n: sb(f"{n}_lo", [128, W], F32R) for n in ("w_pos", "w_neg", "w_one")}
        w1 = [sb("w1_0", [2 * BS + 1, NBLK // 2, 2 * BS]), sb("w1_1", [2 * BS + 1, NBLK, 2 * BS])]
        w2 = [sb("w2_0", [2 * BS + 1, NBLK // 2, 2 * BS]), sb("w2_1", [2 * BS + 1, NBLK, 2 * BS])]
        fring = sb("fring", [128, 2, FCH, C])
        jring = sb("jring", [128, 2, 2, C], F32R)
        with nc.sbuf_tensor("grow", [128, STEPK, C], F32) as grow, nc.sbuf_tensor("z", [128, 2, 2 * C], F32) as z:
            pass
        jmore = sb("jmore", [128, 4, 2, C], F32R)
        zf = z[:, :, :].rearrange("p k (j c) -> p k j c", c=C)
        fslots = [fring[:, 0], fring[:, 1], zf[:, 0], zf[:, 1]]
        jslots = [jring[:, 0], jring[:, 1]] + [jmore[:, k] for k in range(4)]
        xt = sb("xt", [2 * BS + 1, NBLK, NM])
        o1 = sb("o1", [2 * BS + 1, NBLK, NM])
        clip = sb("clip", [112, 2, 2 * NM])
        ss = sb("ss", [112, 4, STEPK * 2, T2])
        spec = sb("spec", [128, STEPK, C])
        et = sb("et", [128, 2, 2, C], F32R)
        ps = ctx.enter_context(nc.psum_tensor("ps", [128, 8, 512], F32))

        c_ld, w_ld, w_ok = sem("const_loaded"), sem("weights_loaded"), sem("weights_ready")
        img_clr = [sem(f"img{s}_cleared") for s in range(SUBS)]
        grow_clr, jmore_clr = sem("grow_cleared"), sem("jmore_cleared")
        ps_clr, wfix = sem("psum_cleared"), sem("weights_cleared")
        x_ld = [[sem(f"x{s}_{k}_loaded") for k in range(NXC)] for s in range(SUBS)]
        y_st = [[sem(f"y{s}_{k}_stored") for k in range(NXC)] for s in range(SUBS)]
        fw_mm, fw_act, fw_dve = sem("fw_product"), sem("fw_copied_act"), sem("fw_copied_dve")
        f_st = [sem(f"f_slot{k}_stored") for k in range(4)]
        mid = []
        for l in range(2):
            m = {n: sem(f"l{l}_{n}") for n in ("a_mm", "b_mm", "c_mm", "d_mm", "t_mm", "e_mm", "a_act", "a_dve",
                                               "b_act", "b_dve", "c_act", "c_dve", "d_clip", "d_ss", "t_act", "t_dve",
                                               "e_hi", "e_lo", "g_ld")}
            m["e_st"] = [sem(f"l{l}_e_slot{k}_stored") for k in range(2)]
            mid.append(m)
        j_ld = [sem(f"j_slot{k}_loaded") for k in range(6)]
        iw_mm, iw_add = sem("iw_product"), sem("iw_added")

        f_adds = [32] * (NFC - 1) + [16]
        f_ring = Ring(4, {(0, 0): (4, f_adds), (0, 1): (2, f_adds), (1, 0): (4, f_adds), (1, 1): (4, f_adds)})
        JC = (-(-HH // 2), HP)
        j_ring = Ring(6, {(0, 0): (2, [16] * JC[0]), (0, 1): (2, [16] * JC[0]),
                          (1, 0): (2, [16] * JC[1]), (1, 1): (6, [16] * JC[1])})
        jobs_of = lambda l, c: min(2 * c + 2, HP) if l == 0 else c + 1
        order = schedule()

        def fw_count(it, l, s):
            return (it * 2 + l) * SUBS + s

        def mid_count(it, s, i):
            return (it * SUBS + s) * STEPS + i

        def inv_rows(l, j):
            if l == 0:
                return [j, H - j] if j else [0]
            return [2 * j, 2 * j + 1][: H - 2 * j]

        def dve_copy(dst, src):
            return nc.vector.tensor_copy(dst, src)

        def dve_relu(dst, src):
            return nc.vector.tensor_scalar(dst, src, 0.0, None, ALU.max)

        def dve_mid(dve, l, s, it):
            m, nb = mid[l], (2, 4)[l]

            def d_ss(n):
                for q in range(nb):
                    dve.wait_ge(m["d_clip"], n * nb + q + 1)
                    rows = (2 * BS, T2 + BS)[l]
                    for r in range(2):
                        part = slice(r * NM, (r + 1) * NM)
                        dst = ss[0:rows, 2 * q + r, 0:STEPK, 0:H] if l == 0 else ss[0:rows, q, r:2 * STEPK:2, 0:H]
                        last = nc.vector.scalar_tensor_tensor(
                            out=dst, in0=clip[0:rows, q, part].rearrange("p (k m) -> p k m", m=H), scalar=2 * LAM,
                            in1=ps[0:rows, 4 + q, part].rearrange("p (k m) -> p k m", m=H), op0=ALU.min, op1=ALU.subtract)
                    last.then_inc(m["d_ss"], 1)

            def e_lo(n):
                for q in range(nb):
                    dve.wait_ge(m["e_hi"], n * nb + q + 1)
                    rows = (T2 + 2 * HH, 2 * H)[l]
                    nc.vector.tensor_tensor(et[0:rows, q % 2, 1, :], ps[0:rows, 4 + q, 0:C],
                                            et[0:rows, q % 2, 0, :].bitcast(F32), ALU.subtract).then_inc(m["e_lo"], 1)

            def first(i):
                n = mid_count(it, s, i)
                for q in range(1, nb, 2):
                    a_copy(dve, dve_copy, l, n, q, "a_dve")
                for q in range(1, nb, 2):
                    b_copy(dve, dve_copy, l, n, q, "b_dve")
                for q in range(1, nb, 2):
                    c_relu(dve, dve_relu, l, n, q, "c_dve")

            def rest(i):
                n = mid_count(it, s, i)
                d_ss(n)
                for q in range(1, nb, 2):
                    t_copy(dve, dve_copy, l, n, q, "t_dve")
                e_lo(n)

            def both(i, second):
                n, o = mid_count(it, s, i), mid_count(it, s, i - 1)
                for q in range(1, nb, 2):
                    a_copy(dve, dve_copy, l, n, q, "a_dve")
                d_ss(o)
                for q in range(1, nb, 2):
                    b_copy(dve, dve_copy, l, n, q, "b_dve")
                for q in range(1, nb, 2):
                    t_copy(dve, dve_copy, l, o, q, "t_dve")
                for q in range(1, nb, 2):
                    c_relu(dve, dve_relu, l, n, q, "c_dve")
                e_lo(o)

            skewed(dve, first, rest, both)

        def copy_fwd(eng, it, l, s, j, half):
            ph, c = fw_count(it, l, s), j // FCH
            rows = T2 + 2 * KWP if 2 * j + 1 < H else 2 * KWP
            if f_ring.vacant(it, (l, s), c) is not None:
                eng.wait_ge(f_st[f_ring.slot((l, s), c)], f_ring.vacant(it, (l, s), c))
            eng.wait_ge(fw_mm, ph * HP + j + 1)
            dst, src = fslots[f_ring.slot((l, s), c)][0:rows, j % FCH, :], ps[0:rows, 4 * half + j % 4, 0:C]
            if j % 2 == 0:
                nc.scalar.activation(dst, src, ACT.Copy).then_inc(fw_act, 1)
            else:
                nc.vector.tensor_copy(dst, src).then_inc(fw_dve, 1)

        def a_copy(eng, copy, l, n, q, done):
            nb = (2, 4)[l]
            eng.wait_ge(mid[l]["a_mm"], n * nb + q + 1)
            if l == 0:
                dst, src = z[0:PR, q, 0:C], ps[0:PR, q, 0:C]
            else:
                dst = z[0:PR, q // 2, :].rearrange("p (b r c) -> p b r c", r=2, c=BS)[:, :, q % 2, :]
                src = ps[0:PR, q, 0:C].rearrange("p (b c) -> p b c", c=BS)
            copy(dst, src).then_inc(mid[l][done], 1)

        def b_copy(eng, copy, l, n, q, done):
            nb = (2, 4)[l]
            eng.wait_ge(mid[l]["b_mm"], n * nb + q + 1)
            pair, b0, bank = (q, 0, 2 + q) if l == 0 else (q // 2, 4 * (q % 2), q)
            dst = xt[0:2 * BS, b0:b0 + 4, pair * 2 * H:(pair + 1) * 2 * H].rearrange("p b (k m) -> p b k m", k=2)
            src = ps[0:2 * BS, bank, :].rearrange("p (b k m) -> p b k m", b=4, k=2)[:, :, :, 0:H]
            copy(dst, src).then_inc(mid[l][done], 1)

        def c_relu(eng, relu, l, n, q, done):
            nb = (2, 4)[l]
            eng.wait_ge(mid[l]["c_mm"], n * nb + q + 1)
            dst = o1[0:2 * BS, 2 * q:2 * q + 2, :].rearrange("p b n -> p (b n)")
            relu(dst, ps[0:2 * BS, q, 0:2 * NM]).then_inc(mid[l][done], 1)

        def t_copy(eng, copy, l, n, q, done):
            nb = (2, 4)[l]
            eng.wait_ge(mid[l]["t_mm"], n * nb + q + 1)
            if l == 0:
                dst, src = spec[0:PR, q, :], ps[0:PR, 6 + q, 0:C]
            else:
                dst = spec[0:PR, q, :].rearrange("p (b c) -> p b c", c=BS)
                src = ps[0:PR, 4 + q, :].rearrange("p (b c) -> p b c", c=T2)[:, :, 0:BS]
            copy(dst, src).then_inc(mid[l][done], 1)

        def act_copy(dst, src):
            return nc.scalar.activation(dst, src, ACT.Copy)

        def act_relu(dst, src):
            return nc.scalar.activation(dst, src, ACT.Relu)

        def stage_copies(eng, kind, copy, relu, l, n, parity):
            name = "act" if parity == 0 else "dve"
            for q in range(parity, (2, 4)[l], 2):
                if kind == "a":
                    a_copy(eng, copy, l, n, q, "a_" + name)
                elif kind == "b":
                    b_copy(eng, copy, l, n, q, "b_" + name)
                elif kind == "c":
                    c_relu(eng, relu, l, n, q, "c_" + name)
                elif kind == "t":
                    t_copy(eng, copy, l, n, q, "t_" + name)

        block = ctx.enter_context(nc.Block())

        @block.sync
        def _(sp):
            def load_g(it, l, s, i):
                rows = scr_f[s].rearrange("h (e k) c -> (h e) k c", e=2)
                sp.dma_start(grow[0:2 * H, :, :], rows[:, i * STEPK:(i + 1) * STEPK, :]).then_inc(mid[l]["g_ld"], 16)

            def load_j(it, l, s, c):
                rows = scr_i[l][s].rearrange("e q h c -> (e q) h c")
                h0, h1 = 2 * c, min(2 * c + 2, (HH, H)[l])
                k = j_ring.slot((l, s), c)
                sp.dma_start(jslots[k][0:4 * KWP, 0:h1 - h0, :].bitcast(F32), rows[:, h0:h1, :]).then_inc(j_ld[k], 16)

            for it in range(ITERS):
                for kind, l, s, *what in order:
                    m, nb, ph = mid[l], (2, 4)[l], fw_count(it, l, s)
                    if kind == "g0":
                        for k, n in f_ring.ended(it, (l, s)):
                            sp.wait_ge(f_st[k], n)
                        if (l, s) == (0, 1):
                            sp.wait_ge(m["a_mm"], (mid_count(it, 0, 0) + STEPS) * nb)
                        sp.wait_ge(grow_clr, it + 1)
                        load_g(it, l, s, 0)
                    if kind == "a" and what[0] + 1 < STEPS:
                        sp.wait_ge(m["a_mm"], (mid_count(it, s, what[0]) + 1) * nb)
                        load_g(it, l, s, what[0] + 1)
                    if kind == "e":
                        i = what[0]
                        for q in range(nb):
                            sp.wait_ge(m["e_lo"], mid_count(it, s, i) * nb + q + 1)
                            if l == 0:
                                for t in range(2):
                                    kk = STEPK * i + 2 * q + t
                                    dst = scr_i[0][s][:, 2 * kk:2 * kk + 2].rearrange("e u h c -> (u h) e c")
                                    sp.dma_start(dst, et[t * T2:t * T2 + 2 * HH, q % 2, :, :].bitcast(F32)).then_inc(m["e_st"][q % 2], 16)
                            else:
                                kk = STEPK * i + q
                                dst = scr_i[1][s][:, 2 * kk:2 * kk + 2].rearrange("e u h c -> (u h) e c")
                                sp.dma_start(dst, et[0:2 * H, q % 2, :, :].bitcast(F32)).then_inc(m["e_st"][q % 2], 16)
                    if kind == "fwd":
                        jobs = what[0]
                        for c in range(jobs[0] // FCH, jobs[-1] // FCH + 1):
                            j0, j1 = c * FCH, min((c + 1) * FCH, HP)
                            sp.wait_ge(fw_act, ph * 12 + (j1 + 1) // 2)
                            if j1 - j0 == FCH:
                                sp.wait_ge(fw_dve, ph * 11 + j1 // 2)
                            k = f_ring.slot((l, s), c)
                            for t in range(2):
                                n = len(range(2 * j0 + t, min(2 * j1, H), 2))
                                if n:
                                    dst = scr_f[s][2 * j0 + t:2 * j0 + t + 2 * n - 1:2].rearrange("h q c -> q h c")
                                    sp.dma_start(dst, fslots[k][t * T2:t * T2 + 2 * KWP, 0:n, :]).then_inc(f_st[k], 16)
                    if kind == "j0":
                        for k in range(2):
                            sp.wait_ge(m["e_st"][k], (mid_count(it, s, 0) + STEPS) * 32)
                        if (l, s) != (0, 0):
                            sp.wait_ge(iw_mm, ph * HP)
                        for c in range(j_ring.uses[l, s][0]):
                            load_j(it, l, s, c)
                    if kind == "inv":
                        R, jobs = j_ring.uses[l, s][0], what[0]
                        for c in range(R, JC[l]):
                            if jobs[0] < jobs_of(l, c - R) <= jobs[-1] + 1:
                                sp.wait_ge(iw_mm, ph * HP + jobs_of(l, c - R))
                                load_j(it, l, s, c)

        @block.gpsimd
        def _(pool):
            clears = [(t[:, :, :], 0.0) for t in (w1[0], w1[1], w2[0], w2[1])]
            clears += [(jring[4 * KWP:128, :, :, :].bitcast(F32), 0.0), (ss[:, :, :, :], 0.0),
                       (xt[2 * BS:2 * BS + 1, :, :], 1.0), (o1[2 * BS:2 * BS + 1, :, :], 1.0)]
            for n, (t, v) in enumerate(clears):
                nc.gpsimd.memset(t, v).then_inc(wfix, 1)
                pool.wait_ge(wfix, n + 1)
            for k in range(NXC):
                nc.gpsimd.memset(img[1][T2:128, k * XCH:(k + 1) * XCH, :], 0.0).then_inc(img_clr[1], 1)
                pool.wait_ge(img_clr[1], k + 1)

            def load_x(b, s, k):
                pool.dma_start(img[s][0:W, k * XCH:(k + 1) * XCH, :],
                               x[b, k * XCH:(k + 1) * XCH].rearrange("h w c -> w h c")).then_inc(x_ld[s][k], 16)

            for s in range(SUBS):
                for k in range(NXC):
                    pool.wait_ge(img_clr[s], k + 1)
                    load_x(s, s, k)
            for it in range(ITERS):
                for s in range(SUBS):
                    ph = fw_count(it, 1, s)
                    for k in range(NXC + 1):
                        if k < NXC:
                            pool.wait_ge(iw_add, ph * HP + min(-(-(k + 1) * XCH // 2), HP))
                            pool.dma_start(out[it * SUBS + s, k * XCH:(k + 1) * XCH].rearrange("h w c -> w h c"),
                                           img[s][0:W, k * XCH:(k + 1) * XCH, :]).then_inc(y_st[s][k], 16)
                        if k > 0 and it + 1 < ITERS:
                            pool.wait_ge(y_st[s][k - 1], 16 * (it + 1))
                            load_x((it + 1) * SUBS + s, s, k - 1)
            for s in range(SUBS):
                for k in range(NXC):
                    pool.wait_ge(y_st[s][k], 16 * ITERS)

        @block.scalar
        def _(act):
            act.dma_start(cst[:, :], const).then_inc(c_ld, 16)
            act.wait_ge(wfix, 4)
            n = 2 * BS
            for t, a, b in ((w1[0], l0_w1, l0_b1), (w2[0], l0_w2, l0_b2)):
                for j in range(2):
                    act.dma_start(t[j * BS:(j + 1) * BS, :, j * BS:(j + 1) * BS],
                                  a[0, j::2].rearrange("n i o -> i n o")).then_inc(w_ld, 16)
                act.dma_start(t[n:n + 1, :, :], b[0:1].rearrange("a (q j) o -> a q (j o)", j=2)).then_inc(w_ld, 16)
            for t, a, b in ((w1[1], l1_w1, l1_b1), (w2[1], l1_w2, l1_b2)):
                for i in range(2):
                    for o in range(2):
                        act.dma_start(t[i * BS:(i + 1) * BS, :, o * BS:(o + 1) * BS],
                                      a[i ^ o].rearrange("n i o -> i n o")).then_inc(w_ld, 16)
                for o in range(2):
                    act.dma_start(t[n:n + 1, :, o * BS:(o + 1) * BS], b[o:o + 1]).then_inc(w_ld, 16)
            act.wait_ge(ps_clr, 1)
            with act.Fori(0, ITERS) as it:
                for kind, l, s, *what in order:
                    m, nb = mid[l], (2, 4)[l]
                    if kind == "fwd":
                        for j in what[0][::2]:
                            copy_fwd(act, it, l, s, j, what[1])
                    if kind in ("a", "b", "c", "t"):
                        stage_copies(act, kind, act_copy, act_relu, l, mid_count(it, s, what[0]), 0)
                    if kind == "d":
                        n, rows = mid_count(it, s, what[0]), (2 * BS, T2 + BS)[l]
                        for q in range(nb):
                            if q >= 2:
                                act.wait_ge(m["d_ss"], n * nb + q - 1)
                            act.wait_ge(m["d_mm"], n * nb + q + 1)
                            act_relu(clip[0:rows, q % 2, :], ps[0:rows, 4 + q, 0:2 * NM]).then_inc(m["d_clip"], 1)
                    if kind == "e":
                        n, rows = mid_count(it, s, what[0]), (T2 + 2 * HH, 2 * H)[l]
                        for q in range(nb):
                            act.wait_ge(m["e_mm"], n * nb + q + 1)
                            if (s, what[0]) != (0, 0) or q >= 2:
                                act.wait_ge(m["e_st"][q % 2], 32 * n + 16 * (q // 2))
                            act_copy(et[0:rows, q % 2, 0, :], ps[0:rows, 4 + q, 0:C]).then_inc(m["e_hi"], 1)

        @block.vector
        def _(dve):
            nc.vector.memset(ps[:, :, :], 0.0).then_inc(ps_clr, 1)
            for k in range(NXC):
                nc.vector.memset(img[0][T2:128, k * XCH:(k + 1) * XCH, :], 0.0).then_inc(img_clr[0], 1)
            dve.wait_ge(c_ld, 16)
            for n in iw_hi:
                nc.vector.tensor_copy(iw_hi[n][:, :], K[n]).then_inc(w_ok, 1)
            dve.wait_ge(w_ld, 16 * 18)
            dve.wait_ge(w_ok, 3)
            for n in iw_hi:
                nc.vector.tensor_tensor(iw_lo[n][:, :], K[n], iw_hi[n][:, :].bitcast(F32), ALU.subtract).then_inc(w_ok, 1)
            for t in (w1[1], w2[1]):
                v = t[0:2 * BS, :, 0:BS]
                nc.vector.tensor_scalar(v, v, K["sign"][0:2 * BS, :], None, ALU.mult).then_inc(w_ok, 1)
            for t in w2:
                v = t[2 * BS:2 * BS + 1, :, :]
                nc.vector.tensor_scalar(v, v, LAM, None, ALU.add).then_inc(w_ok, 1)
            with dve.Fori(0, ITERS) as it:
                nc.vector.memset(grow[T2:128, :, :], 0.0).then_inc(grow_clr, 1)
                for kind, l, s, *what in order:
                    m, nb, ph = mid[l], (2, 4)[l], fw_count(it, l, s)
                    if (kind, l, s) == ("j0", 1, 1):
                        dve.wait_ge(m["e_mm"], (mid_count(it, s, 0) + STEPS) * nb)
                        nc.vector.memset(jmore[4 * KWP:128, :, :, :].bitcast(F32), 0.0).then_inc(jmore_clr, 1)
                    if kind == "fwd":
                        for j in what[0][1::2]:
                            copy_fwd(dve, it, l, s, j, what[1])
                    if kind in ("a", "b", "c", "t"):
                        stage_copies(dve, kind, dve_copy, dve_relu, l, mid_count(it, s, what[0]), 1)
                    if kind == "d":
                        n, rows = mid_count(it, s, what[0]), (2 * BS, T2 + BS)[l]
                        for q in range(nb):
                            dve.wait_ge(m["d_clip"], n * nb + q + 1)
                            for r in range(2):
                                part = slice(r * NM, (r + 1) * NM)
                                dst = ss[0:rows, 2 * q + r, 0:STEPK, 0:H] if l == 0 else ss[0:rows, q, r:2 * STEPK:2, 0:H]
                                last = nc.vector.scalar_tensor_tensor(
                                    out=dst, in0=clip[0:rows, q % 2, part].rearrange("p (k m) -> p k m", m=H), scalar=2 * LAM,
                                    in1=ps[0:rows, 4 + q, part].rearrange("p (k m) -> p k m", m=H), op0=ALU.min, op1=ALU.subtract)
                            last.then_inc(m["d_ss"], 1)
                    if kind == "e":
                        n, rows = mid_count(it, s, what[0]), (T2 + 2 * HH, 2 * H)[l]
                        for q in range(nb):
                            dve.wait_ge(m["e_hi"], n * nb + q + 1)
                            nc.vector.tensor_tensor(et[0:rows, q % 2, 1, :], ps[0:rows, 4 + q, 0:C],
                                                    et[0:rows, q % 2, 0, :].bitcast(F32), ALU.subtract).then_inc(m["e_lo"], 1)
                    if kind == "inv":
                        for j in what[0]:
                            dve.wait_ge(iw_mm, ph * HP + j + 1)
                            hs = inv_rows(l, j)
                            bank = 4 * what[1] + 2 * (j % 2)
                            if len(hs) == 1:
                                y, p = img[s][0:W, hs[0], :], ps[0:W, bank, 0:C]
                            else:
                                y, p = img[s][0:W, hs[0]:hs[1] + 1:hs[1] - hs[0], :], ps[0:W, bank:bank + 2, 0:C]
                            nc.vector.tensor_tensor(y, p, y, ALU.add).then_inc(iw_add, 1)

        @block.tensor
        def _(pe):
            mm = nc.tensor.matmul
            pe.wait_ge(c_ld, 16)
            pe.wait_ge(ps_clr, 1)
            pe.wait_ge(wfix, 8)

            tenant = [None, None]

            def vacate(half):
                for sem_, n in tenant[half] or []:
                    pe.wait_ge(sem_, n)

            def fwd(l, s, it, jobs, half):
                ph = fw_count(it, l, s)
                vacate(half)
                for j in jobs:
                    for k in range(NXC):
                        if l == 0 and 2 * j <= k * XCH < 2 * j + 2:
                            pe.wait_ge(x_ld[s][k], 16 * (it + 1))
                    if l == 1 and j == 0:
                        pe.wait_ge(iw_add, (ph - 1) * HP)
                    for t in range(2):
                        h = 2 * j + t
                        if h < H:
                            last = mm(ps[t * T2:t * T2 + 2 * KWP, 4 * half + j % 4, 0:C], K["w_fwd"], img[s][:, h, :], start=True, stop=True)
                    last.then_inc(fw_mm, 1)
                tenant[half] = [(fw_act, ph * 12 + jobs[-1] // 2 + 1)]
                if len(jobs) > 1:
                    tenant[half].append((fw_dve, ph * 11 + (jobs[-1] + 1) // 2))

            def inv(l, s, it, jobs, half):
                ph = fw_count(it, l, s)
                vacate(half)
                if (l, s) == (1, 1):
                    pe.wait_ge(jmore_clr, it + 1)
                for j in jobs:
                    c, at = (j // 2, j % 2) if l == 0 else (j, 0)
                    k = j_ring.slot((l, s), c)
                    if at == 0:
                        pe.wait_ge(j_ld[k], j_ring.landed(it, (l, s), c))
                    for t, _h in enumerate(inv_rows(l, j)):
                        n = ("w_pos", "w_neg")[t] if l == 0 else "w_one"
                        bank, row = 4 * half + 2 * (j % 2) + t, jslots[k][:, at if l == 0 else t, :]
                        mm(ps[0:W, bank, 0:C], iw_hi[n][:, :], row, start=True, stop=False)
                        last = mm(ps[0:W, bank, 0:C], iw_lo[n][:, :], row, start=False, stop=True)
                    last.then_inc(iw_mm, 1)
                tenant[half] = [(iw_add, ph * HP + jobs[-1] + 1)]

            def stage(kind, l, s, it, i):
                m, nb = mid[l], (2, 4)[l]
                half = nb // 2

                def a_h(n):
                    pe.wait_ge(m["g_ld"], 16 * (n + 1))
                    vacate(0)
                    for q in range(nb):
                        pair, name = (q, "h_cas") if l == 0 else (q // 2, ("h_re", "h_im")[q % 2])
                        for t in range(2):
                            last = mm(ps[t * T2:t * T2 + H, q, 0:C], K[name], grow[:, 2 * pair + t, :], start=True, stop=True)
                        last.then_inc(m["a_mm"], 1)

                def b_transpose(n):
                    for q in range(nb):
                        pair, b0, bank = (q, 0, 2 + q) if l == 0 else (q // 2, 4 * (q % 2), q)
                        if l == 0:
                            pe.wait_ge(m[("a_act", "a_dve")[q]], n + 1)
                        elif q % 2 == 0:
                            pe.wait_ge(m["a_act"], n * 2 + pair + 1)
                            pe.wait_ge(m["a_dve"], n * 2 + pair + 1)
                        for b in range(4):
                            last = nc.tensor.transpose(ps[0:2 * BS, bank, b * 128:b * 128 + PR],
                                                       z[0:PR, pair, (b0 + b) * 2 * BS:(b0 + b + 1) * 2 * BS], K["ident"][0:PR, 0:PR])
                        last.then_inc(m["b_mm"], 1)

                def c_block(n):
                    pe.wait_ge(m["b_act"], (n + 1) * half)
                    pe.wait_ge(m["b_dve"], (n + 1) * half)
                    for q in range(nb):
                        for b in range(2):
                            last = mm(ps[0:2 * BS, q, b * NM:(b + 1) * NM], w1[l][:, 2 * q + b, :], xt[:, 2 * q + b, :], start=True, stop=True)
                        last.then_inc(m["c_mm"], 1)
                    tenant[0] = [(m["c_act"], (n + 1) * half), (m["c_dve"], (n + 1) * half)]

                def d_block(n):
                    pe.wait_ge(m["c_act"], (n + 1) * half)
                    pe.wait_ge(m["c_dve"], (n + 1) * half)
                    vacate(1)
                    for q in range(nb):
                        for r in range(2):
                            if l == 0:
                                last = mm(ps[0:2 * BS, 4 + q, r * NM:(r + 1) * NM], w2[0][:, 2 * q + r, :], o1[:, 2 * q + r, :], start=True, stop=True)
                            else:
                                for t in range(2):
                                    last = mm(ps[t * T2:t * T2 + BS, 4 + q, r * NM:(r + 1) * NM],
                                              w2[1][:, 2 * q + t, r * BS:(r + 1) * BS], o1[:, 2 * q + t, :], start=True, stop=True)
                        last.then_inc(m["d_mm"], 1)

                def t_transpose(n):
                    pe.wait_ge(m["d_ss"], (n + 1) * nb)
                    for q in range(nb):
                        rows, wide, bank = (2 * BS, 2 * BS, 6 + q) if l == 0 else (T2 + BS, 128, 4 + q)
                        for b in range(4):
                            modes = ss[0:rows, b, 2 * q:2 * q + 2, :].rearrange("p k m -> p (k m)")[:, 0:PR]
                            last = nc.tensor.transpose(ps[0:PR, bank, b * wide:b * wide + rows], modes, K["ident"][0:rows, 0:rows])
                        last.then_inc(m["t_mm"], 1)

                def e_h(n):
                    for q in range(nb):
                        eng = ("t_act", "t_dve")[q % 2]
                        pe.wait_ge(m[eng], n * half + q // 2 + 1)
                        if l == 0:
                            for t in range(2):
                                last = mm(ps[t * T2:t * T2 + 2 * HH, 4 + q, 0:C], K[("u0_lo", "u0_hi")[t]][0:PR, :],
                                          spec[0:PR, q, :], start=True, stop=True)
                        else:
                            last = mm(ps[0:2 * H, 4 + q, 0:C], K["u1"][0:PR, :], spec[0:PR, q, :], start=True, stop=True)
                        last.then_inc(m["e_mm"], 1)
                    tenant[1] = [(m["e_lo"], (n + 1) * nb)]

                {"a": a_h, "b": b_transpose, "c": c_block, "d": d_block, "t": t_transpose, "e": e_h}[kind](mid_count(it, s, i))

            with pe.Fori(0, ITERS) as it:
                for n, (kind, l, s, *what) in enumerate(order):
                    if kind == "fwd":
                        fwd(l, s, it, *what)
                    elif kind == "inv":
                        inv(l, s, it, *what)
                    elif kind in "abcdte":
                        if kind == "c" and l == 0 and s == 0 and what[0] == 0:
                            pe.wait_ge(w_ok, 10)
                        stage(kind, l, s, it, *what)
                pe.wait_ge(iw_add, (fw_count(it, 1, 1) + 1) * HP)
    return nc


def kernel(**inputs):
    import concourse.bacc as bacc
    from concourse.bass_utils import run_bass_kernel_spmd

    nc = bacc.Bacc("TRN2", target_bir_lowering=False, num_devices=1)
    const, where = constants()
    arrays, args = {}, []
    names = ["x"] + [f"L{l}_conv_{n}" for l in range(2) for n in ("w1", "b1", "w2", "b2")]
    for name in names:
        arrays[name] = np.ascontiguousarray(inputs[name])
    arrays["const"] = const
    for name, a in arrays.items():
        args.append(nc.dram_tensor(name, a.shape, mybir.dt.from_np(a.dtype), kind="ExternalInput").ap())
    out = nc.dram_tensor("y", (B, H, W, C), F32, kind="ExternalOutput").ap()
    spectral_layers(nc, *args, out, where)
    r = run_bass_kernel_spmd(nc, [arrays], core_ids=[0])
    return r.results[0]["y"]
```

```python
from contextlib import ExitStack

import numpy as np

import concourse.bass as bass
from concourse import mybir

F32 = mybir.dt.float32
F32R = mybir.dt.float32r
ALU = mybir.AluOpType
ACT = mybir.ActivationFunctionType

B, H, W, C = 4, 45, 90, 384
KW = (H // 2 + 1)
KWP = KW + 1
BS = 48
NBLK = C // BS
LAM = 0.01
HH = H // 2 + 1
T2 = 64
PR = T2 + H
SUBS = 2
ITERS = B // SUBS
STEPK = 4
STEPS = KWP // STEPK
NM = STEPK * H
HP = (H + 1) // 2
FCH = 2
PF = T2 + 2 * KWP
NFC = -(-HP // FCH)
XCH = 5
NXC = H // XCH
SHARES = {"a": (("act", "dve"), ("act", "dve", "act", "dve")), "b": (("act", "dve"), ("act", "dve", "act", "dve")),
          "c": (("act", "act"), ("act", "dve", "act", "dve")), "t": (("act", "dve"), ("act", "dve", "act", "dve"))}


def constants():
    w, kw = np.arange(W), np.arange(KWP)
    h, kh = np.arange(H), np.arange(H)
    norm = 1 / np.sqrt(H * W)
    live = (kw < KW)
    parts = {}

    def put(name, rows):
        full = np.zeros((128, rows.shape[1]))
        full[: rows.shape[0]] = rows
        parts[name] = full

    aw = 2 * np.pi * np.outer(w, kw) / W
    put("w_fwd", np.concatenate([np.cos(aw) * live, np.sin(aw) * live], 1))
    ah = 2 * np.pi * np.outer(h, kh) / H
    co, si = np.cos(ah) * norm, np.sin(ah) * norm
    pair = lambda a, b: np.stack([a, b], 1).reshape(2 * H, H)
    put("h_cas", pair(co + si, co - si))
    put("h_re", pair(co, -si))
    put("h_im", pair(-si, -co))
    ci, sn = -np.cos(ah.T) * norm, -np.sin(ah.T) * norm
    real = np.concatenate([ci[:, :HH], sn[:, :HH]], 1)
    up = np.zeros((PR, 2 * HH))
    up[T2:] = real
    put("u0_lo", real)
    put("u0_hi", up)
    both = np.zeros((PR, 2 * H))
    both[:H] = np.concatenate([ci, sn], 1)
    both[T2:] = np.concatenate([-sn, ci], 1)
    put("u1", both)
    for name, weight, sign in (("w_pos", live * 1.0, -1), ("w_neg", live * 1.0, 1), ("w_one", live * np.where(kw == 0, 1.0, 2.0), -1)):
        rows = np.stack([np.cos(aw.T) * weight[:, None], sign * np.sin(aw.T) * weight[:, None]], 1).reshape(2 * KWP, W)
        put(name, np.concatenate([rows, rows], 0))
    put("ident", np.eye(128))
    sign = np.ones((128, 1))
    sign[BS:2 * BS] = -1
    put("sign", sign)
    at, where = 0, {}
    for name, a in parts.items():
        where[name] = (at, a.shape[1])
        at += a.shape[1]
    return np.concatenate(list(parts.values()), 1).astype(np.float32), where


class Ring:

    def __init__(self, uses):
        self.uses, self.count, self.before = uses, {}, {}
        total = {}
        for phase, (slots, adds) in uses.items():
            for c, add in enumerate(adds):
                k = slots[c % len(slots)]
                self.before[phase, c] = total.get(k, 0)
                self.count[phase, c] = total[k] = total.get(k, 0) + add

    def slots(self, phase):
        return self.uses[phase][0]

    def slot(self, phase, c):
        return self.slots(phase)[c % len(self.slots(phase))]

    def landed(self, phase, c):
        return self.count[phase, c]

    def vacant(self, phase, c):
        return self.before[phase, c]

    def ended(self, phase):
        last = {self.slot(phase, c): self.count[phase, c] for c in range(len(self.uses[phase][1]))}
        return list(last.items())


def schedule():
    order, half = [], [1]

    def groups(it, kind, l, s, n=None):
        n = n or (4 if kind == "fwd" else 2)
        return [(it, kind, l, s, tuple(range(j, min(j + n, HP)))) for j in range(0, HP, n)]

    def plain(gs):
        for g in gs:
            half[0] ^= 1
            order.append(g + (half[0],))

    def middle(it, l, s, light, late=(), g0=None, j0=None):
        light = list(light)

        def gap(h):
            if light:
                order.append(light.pop(0) + (h,))

        for i in range(STEPS):
            order.append((it, "a", l, s, i))
            if i == 0 and j0:
                order.append(j0)
            if i:
                gap(1)
            order.append((it, "b", l, s, i))
            if i:
                order.append((it, "d", l, s, i - 1))
            order.append((it, "c", l, s, i))
            if i:
                order.append((it, "t", l, s, i - 1))
            gap(0)
            if i:
                order.append((it, "e", l, s, i - 1))
        half[0] = 0
        plain(light + list(late))
        if g0:
            order.append(g0)
        order.extend((it, k, l, s, STEPS - 1) for k in "dte")

    plain(groups(0, "fwd", 0, 0))
    order.append((0, "g0", 0, 0))
    for it in range(ITERS):
        if it == 0:
            middle(it, 0, 0, groups(it, "fwd", 0, 1, 2), g0=(it, "g0", 0, 1))
        else:
            middle(it, 0, 0, groups(it - 1, "inv", 1, 1), groups(it, "fwd", 0, 1), (it, "g0", 0, 1), (it - 1, "j0", 1, 1))
        middle(it, 0, 1, groups(it, "inv", 0, 0), groups(it, "fwd", 1, 0), (it, "g0", 1, 0), (it, "j0", 0, 0))
        middle(it, 1, 0, groups(it, "inv", 0, 1), groups(it, "fwd", 1, 1), (it, "g0", 1, 1), (it, "j0", 0, 1))
        if it + 1 < ITERS:
            middle(it, 1, 1, groups(it, "inv", 1, 0), groups(it + 1, "fwd", 0, 0), (it + 1, "g0", 0, 0), (it, "j0", 1, 0))
        else:
            middle(it, 1, 1, groups(it, "inv", 1, 0), j0=(it, "j0", 1, 0))
    order.append((ITERS - 1, "j0", 1, 1))
    plain(groups(ITERS - 1, "inv", 1, 1))
    return order


def spectral_layers(nc, x, l0_w1, l0_b1, l0_w2, l0_b2, l1_w1, l1_b1, l1_w2, l1_b2, const, out, where):
    ctx = ExitStack()
    with ctx:
        sb = lambda name, shape, dt=F32: ctx.enter_context(nc.sbuf_tensor(name, shape, dt))
        sem = lambda name: ctx.enter_context(nc.semaphore(name))

        scr_f = [nc.dram_tensor(f"scr_f{s}", (H, 2 * KWP, C), F32, kind="Internal").ap() for s in range(SUBS)]
        scr_i = [[nc.dram_tensor(f"scr_i{l}{s}", (2, 2 * KWP, (HH, H)[l], C), F32, kind="Internal").ap()
                  for s in range(SUBS)] for l in range(2)]

        img = [sb(f"img{s}", [128, H, C]) for s in range(SUBS)]
        cst = sb("cst", [128, const.shape[1]])
        K = {n: cst[:, a:a + m] for n, (a, m) in where.items()}
        iw_hi = {n: sb(f"{n}_hi", [128, W], F32R) for n in ("w_pos", "w_neg", "w_one")}
        iw_lo = {n: sb(f"{n}_lo", [128, W], F32R) for n in ("w_pos", "w_neg", "w_one")}
        w1 = [sb("w1_0", [2 * BS + 1, NBLK // 2, 2 * BS]), sb("w1_1", [PF, NBLK, 2 * BS])]
        w2 = [sb("w2_0", [2 * BS + 1, NBLK // 2, 2 * BS]), sb("w2_1", [PF, NBLK, 2 * BS])]
        jring = sb("jring", [128, 2, 2, C], F32R)
        grow = sb("grow", [128, STEPK, C])
        z = sb("z", [128, 2, 2 * C])
        fslots = [z[:, k, :].rearrange("p (j c) -> p j c", c=C) for k in range(2)]
        fslots += [grow[:, 2 * k:2 * k + 2, :] for k in range(2)] + [t[:, :, :].rearrange("p (j q) c -> p j (q c)", j=2) for t in (w1[1], w2[1])]
        xt = sb("xt", [2 * BS + 1, NBLK, NM])
        o1 = sb("o1", [2 * BS + 1, NBLK, NM])
        clip = sb("clip", [112, 2, 2 * NM])
        ss = sb("ss", [112, 4, STEPK * 2, T2])
        spec = sb("spec", [128, STEPK, C])
        et = sb("et", [128, 4, 2, C], F32R)
        jslots = [jring[:, k] for k in range(2)] + [et[:, k] for k in range(4)]
        ps = ctx.enter_context(nc.psum_tensor("ps", [128, 8, 512], F32))

        c_ld = sem("const_loaded")
        w_ld = [sem(f"l{l}_weights_loaded") for l in range(2)]
        w_ok = [sem(f"l{l}_weights_ready") for l in range(2)]
        iw_ok = sem("inverse_matrices_split")
        img0_clr = [sem("img0_even_chunks_cleared"), sem("img0_odd_chunks_cleared")]
        img1_clr, grow_clr, et_clr = sem("img1_cleared"), sem("grow_cleared"), sem("et_cleared")
        ps_clr, wfix = [sem("psum_low_cleared"), sem("psum_high_cleared")], sem("pool_cleared")
        x_first = [sem(f"x_first_{k}_loaded") for k in range(NXC)]
        x_ld = [[sem(f"x{s}_{k}_loaded") for k in range(NXC)] for s in range(SUBS)]
        y_st = [[sem(f"y{s}_{k}_stored") for k in range(NXC)] for s in range(SUBS)]
        fw_mm, fw_copy = sem("fw_product"), sem("fw_copied")
        f_st = [sem(f"f_slot{k}_stored") for k in range(6)]
        mid = []
        for l in range(2):
            m = {n: sem(f"l{l}_{n}") for n in ("a_mm", "b_mm", "c_mm", "d_mm", "t_mm", "e_mm", "a_act", "a_dve",
                                               "b_act", "b_dve", "c_act", "c_dve", "d_clip", "d_ss", "t_act", "t_dve",
                                               "e_hi", "e_lo", "g_ld")}
            m["e_st"] = [sem(f"l{l}_e_slot{k}_stored") for k in range((2, 4)[l])]
            mid.append(m)
        j_ld = [sem(f"j_slot{k}_loaded") for k in range(6)]
        iw_mm, iw_add = sem("iw_product"), sem("iw_added")

        f_adds = [32] * (NFC - 1) + [16]
        phases = [(it, l, s) for it in range(ITERS) for l in range(2) for s in range(SUBS)]
        f_ring = Ring({p: ((4, 5) if p == (0, 0, 1) else (0, 1, 2, 3), f_adds) for p in phases})
        JC = (-(-HH // 2), HP)
        j_slots = lambda p: tuple(range(6)) if p == phases[-1] else (0, 1, 4, 5) if p[1:] in ((0, 0), (1, 1)) else (0, 1)
        j_ring = Ring({p: (j_slots(p), [16] * JC[p[1]]) for p in phases})
        jobs_of = lambda l, c: min(2 * c + 2, HP) if l == 0 else c + 1
        order = schedule()

        def fw_count(it, l, s):
            return (it * 2 + l) * SUBS + s

        def mid_count(it, s, i):
            return (it * SUBS + s) * STEPS + i

        def x_loaded(it, s, k):
            if s == 0:
                return (x_ld[0][k], 16 * it) if it else (x_first[k], 16)
            return x_ld[s][k], 16 * (it + 1)

        def inv_rows(l, j):
            if l == 0:
                return [j, H - j] if j else [0]
            return [2 * j, 2 * j + 1][: H - 2 * j]

        def dve_copy(dst, src):
            return nc.vector.tensor_copy(dst, src)

        def dve_relu(dst, src):
            return nc.vector.tensor_scalar(dst, src, 0.0, None, ALU.max)

        def banks_of(engine, kind, l):
            return [q for q, e in enumerate(SHARES[kind][l]) if e == engine]

        def copied(kind, l, n, banks):
            waits = []
            for engine in ("act", "dve"):
                mine = banks_of(engine, kind, l)
                last = [i for i, q in enumerate(mine) if q in banks]
                if last:
                    waits.append((mid[l][f"{kind}_{engine}"], n * len(mine) + last[-1] + 1))
            return waits

        def copy_fwd(eng, it, l, s, j, half):
            ph, c = fw_count(it, l, s), j // FCH
            rows = PF if 2 * j + 1 < H else 2 * KWP
            k = f_ring.slot((it, l, s), c)
            if f_ring.vacant((it, l, s), c):
                eng.wait_ge(f_st[k], f_ring.vacant((it, l, s), c))
            eng.wait_ge(fw_mm, ph * HP + j + 1)
            dst, src = fslots[k][0:rows, j % FCH, :], ps[0:rows, 4 * half + j % 4, 0:C]
            nc.scalar.activation(dst, src, ACT.Copy).then_inc(fw_copy, 1)

        def load_x(eng, b, s, k, loaded):
            eng.dma_start(img[s][0:W, k * XCH:(k + 1) * XCH, :],
                          x[b, k * XCH:(k + 1) * XCH].rearrange("h w c -> w h c")).then_inc(loaded, 16)

        def a_copy(eng, copy, l, n, q, done):
            nb = (2, 4)[l]
            eng.wait_ge(mid[l]["a_mm"], n * nb + q + 1)
            if l == 0:
                dst, src = z[0:PR, q, 0:C], ps[0:PR, q, 0:C]
            else:
                dst = z[0:PR, q // 2, :].rearrange("p (b r c) -> p b r c", r=2, c=BS)[:, :, q % 2, :]
                src = ps[0:PR, q, 0:C].rearrange("p (b c) -> p b c", c=BS)
            copy(dst, src).then_inc(mid[l][done], 1)

        def b_copy(eng, copy, l, n, q, done):
            nb = (2, 4)[l]
            eng.wait_ge(mid[l]["b_mm"], n * nb + q + 1)
            pair, b0, bank = (q, 0, 2 + q) if l == 0 else (q // 2, 4 * (q % 2), q)
            dst = xt[0:2 * BS, b0:b0 + 4, pair * 2 * H:(pair + 1) * 2 * H].rearrange("p b (k m) -> p b k m", k=2)
            src = ps[0:2 * BS, bank, :].rearrange("p (b k m) -> p b k m", b=4, k=2)[:, :, :, 0:H]
            copy(dst, src).then_inc(mid[l][done], 1)

        def c_relu(eng, relu, l, n, q, done):
            nb = (2, 4)[l]
            eng.wait_ge(mid[l]["c_mm"], n * nb + q + 1)
            dst = o1[0:2 * BS, 2 * q:2 * q + 2, :].rearrange("p b n -> p (b n)")
            relu(dst, ps[0:2 * BS, q, 0:2 * NM]).then_inc(mid[l][done], 1)

        def t_copy(eng, copy, l, n, q, done):
            nb = (2, 4)[l]
            eng.wait_ge(mid[l]["t_mm"], n * nb + q + 1)
            if l == 0:
                dst, src = spec[0:PR, q, :], ps[0:PR, 6 + q, 0:C]
            else:
                dst = spec[0:PR, q, :].rearrange("p (b c) -> p b c", c=BS)
                src = ps[0:PR, 4 + q, :].rearrange("p (b c) -> p b c", c=T2)[:, :, 0:BS]
            copy(dst, src).then_inc(mid[l][done], 1)

        def act_copy(dst, src):
            return nc.scalar.activation(dst, src, ACT.Copy)

        def act_relu(dst, src):
            return nc.scalar.activation(dst, src, ACT.Relu)

        def stage_copies(eng, name, kind, copy, relu, l, n):
            for q in banks_of(name, kind, l):
                if kind == "a":
                    a_copy(eng, copy, l, n, q, "a_" + name)
                elif kind == "b":
                    b_copy(eng, copy, l, n, q, "b_" + name)
                elif kind == "c":
                    c_relu(eng, relu, l, n, q, "c_" + name)
                elif kind == "t":
                    t_copy(eng, copy, l, n, q, "t_" + name)

        block = ctx.enter_context(nc.Block())

        @block.sync
        def _(sp):
            def load_g(it, l, s, i):
                rows = scr_f[s].rearrange("h (e k) c -> (h e) k c", e=2)
                sp.dma_start(grow[0:2 * H, :, :], rows[:, i * STEPK:(i + 1) * STEPK, :]).then_inc(mid[l]["g_ld"], 16)

            def load_j(it, l, s, c):
                rows = scr_i[l][s].rearrange("e q h c -> (e q) h c")
                h0, h1 = 2 * c, min(2 * c + 2, (HH, H)[l])
                k = j_ring.slot((it, l, s), c)
                sp.dma_start(jslots[k][0:4 * KWP, 0:h1 - h0, :].bitcast(F32), rows[:, h0:h1, :]).then_inc(j_ld[k], 16)

            sp.dma_start(cst[:, :], const).then_inc(c_ld, 16)
            for k in range(NXC):
                sp.wait_ge(img0_clr[k % 2], k // 2 + 1)
                load_x(sp, 0, 0, k, x_first[k])
            for it, kind, l, s, *what in order:
                m, nb, ph = mid[l], (2, 4)[l], fw_count(it, l, s)
                if kind == "g0":
                    for k, n in f_ring.ended((it, l, s)):
                        sp.wait_ge(f_st[k], n)
                    if (l, s) == (0, 1):
                        sp.wait_ge(m["a_mm"], (mid_count(it, 0, 0) + STEPS) * nb)
                    load_g(it, l, s, 0)
                if kind == "a" and what[0] + 1 < STEPS:
                    sp.wait_ge(m["a_mm"], (mid_count(it, s, what[0]) + 1) * nb)
                    load_g(it, l, s, what[0] + 1)
                if kind == "e":
                    i = what[0]
                    for q in range(nb):
                        sp.wait_ge(m["e_lo"], mid_count(it, s, i) * nb + q + 1)
                        if l == 0:
                            for t in range(2):
                                kk = STEPK * i + 2 * q + t
                                dst = scr_i[0][s][:, 2 * kk:2 * kk + 2].rearrange("e u h c -> (u h) e c")
                                sp.dma_start(dst, et[t * T2:t * T2 + 2 * HH, q, :, :].bitcast(F32)).then_inc(m["e_st"][q], 16)
                        else:
                            kk = STEPK * i + q
                            dst = scr_i[1][s][:, 2 * kk:2 * kk + 2].rearrange("e u h c -> (u h) e c")
                            sp.dma_start(dst, et[0:2 * H, q, :, :].bitcast(F32)).then_inc(m["e_st"][q], 16)
                if kind == "fwd":
                    jobs = what[0]
                    for c in range(jobs[0] // FCH, jobs[-1] // FCH + 1):
                        j0, j1 = c * FCH, min((c + 1) * FCH, HP)
                        sp.wait_ge(fw_copy, ph * HP + j1)
                        k = f_ring.slot((it, l, s), c)
                        for t in range(2):
                            n = len(range(2 * j0 + t, min(2 * j1, H), 2))
                            if n:
                                dst = scr_f[s][2 * j0 + t:2 * j0 + t + 2 * n - 1:2].rearrange("h q c -> q h c")
                                sp.dma_start(dst, fslots[k][t * T2:t * T2 + 2 * KWP, 0:n, :]).then_inc(f_st[k], 16)
                if kind == "j0":
                    for e_st in m["e_st"]:
                        sp.wait_ge(e_st, (mid_count(it, s, 0) + STEPS) * (32, 16)[l])
                    if (l, s) != (0, 0):
                        sp.wait_ge(iw_mm, ph * HP)
                    for c in range(len(j_ring.slots((it, l, s)))):
                        load_j(it, l, s, c)
                if kind == "inv":
                    R, jobs = len(j_ring.slots((it, l, s))), what[0]
                    for c in range(R, JC[l]):
                        if jobs[0] < jobs_of(l, c - R) <= jobs[-1] + 1:
                            sp.wait_ge(iw_mm, ph * HP + jobs_of(l, c - R))
                            load_j(it, l, s, c)

        def load_weights(pool, l):
            n = 2 * BS
            if l == 0:
                for t, a, b in ((w1[0], l0_w1, l0_b1), (w2[0], l0_w2, l0_b2)):
                    for j in range(2):
                        pool.dma_start(t[j * BS:(j + 1) * BS, :, j * BS:(j + 1) * BS],
                                       a[0, j::2].rearrange("n i o -> i n o")).then_inc(w_ld[0], 16)
                    pool.dma_start(t[n:n + 1, :, :], b[0:1].rearrange("a (q j) o -> a q (j o)", j=2)).then_inc(w_ld[0], 16)
            else:
                for t, a, b in ((w1[1], l1_w1, l1_b1), (w2[1], l1_w2, l1_b2)):
                    for i in range(2):
                        for o in range(2):
                            pool.dma_start(t[i * BS:(i + 1) * BS, :, o * BS:(o + 1) * BS],
                                           a[i ^ o].rearrange("n i o -> i n o")).then_inc(w_ld[1], 16)
                    for o in range(2):
                        pool.dma_start(t[n:n + 1, :, o * BS:(o + 1) * BS], b[o:o + 1]).then_inc(w_ld[1], 16)

        @block.gpsimd
        def _(pool):
            cleared = [0]

            def clear(t, v, which=None):
                if which is None:
                    nc.gpsimd.memset(t, v).then_inc(wfix, 1)
                    cleared[0] += 1
                    pool.wait_ge(wfix, cleared[0])
                else:
                    nc.gpsimd.memset(t, v).then_inc(which[0], 1)
                    pool.wait_ge(which[0], which[1])

            for k in range(0, NXC, 2):
                clear(img[0][T2:128, k * XCH:(k + 1) * XCH, :], 0.0, (img0_clr[0], k // 2 + 1))
            for t in (w1[0], w2[0], ss):
                clear(t[:], 0.0)
            for t in (xt, o1):
                clear(t[2 * BS:2 * BS + 1, :, :], 1.0)
            load_weights(pool, 0)
            clear(jring[4 * KWP:128, :, :, :].bitcast(F32), 0.0)
            pool.wait_ge(w_ld[0], 16 * 6)
            v = w2[0][2 * BS:2 * BS + 1, :, :]
            nc.gpsimd.tensor_scalar(v, v, LAM, None, ALU.add).then_inc(w_ok[0], 1)
            pool.wait_ge(c_ld, 16)
            pool.wait_ge(w_ok[0], 1)
            for n in iw_hi:
                nc.gpsimd.tensor_copy(iw_hi[n][:, :], K[n]).then_inc(iw_ok, 1)
            pool.wait_ge(iw_ok, 3)
            for n in iw_hi:
                nc.gpsimd.tensor_tensor(iw_lo[n][:, :], K[n], iw_hi[n][:, :].bitcast(F32), ALU.subtract).then_inc(iw_ok, 1)
            pool.wait_ge(mid[0]["g_ld"], 16)
            for k in range(NXC):
                pool.wait_ge(img1_clr, k + 1)
                if k >= 4:
                    pool.wait_ge(mid[0]["a_mm"], ((k - 4) // 2 + 1) * 2)
                load_x(pool, 1, 1, k, x_ld[1][k])
            for k, n in f_ring.ended((0, 0, 1)):
                pool.wait_ge(f_st[k], n)
            for t in (w1[1], w2[1]):
                clear(t[0:2 * BS + 1], 0.0)
            load_weights(pool, 1)
            pool.wait_ge(iw_ok, 6)
            pool.wait_ge(w_ld[1], 16 * 12)
            for t in (w1[1], w2[1]):
                v = t[0:2 * BS, :, 0:BS]
                nc.gpsimd.tensor_scalar(v, v, K["sign"][0:2 * BS, :], None, ALU.mult).then_inc(w_ok[1], 1)
            pool.wait_ge(w_ok[1], 2)
            v = w2[1][2 * BS:2 * BS + 1, :, :]
            nc.gpsimd.tensor_scalar(v, v, LAM, None, ALU.add).then_inc(w_ok[1], 1)

            for it in range(ITERS):
                for s in range(SUBS):
                    ph = fw_count(it, 1, s)
                    for k in range(NXC + 1):
                        if k < NXC:
                            pool.wait_ge(iw_add, ph * HP + min(-(-(k + 1) * XCH // 2), HP))
                            pool.dma_start(out[it * SUBS + s, k * XCH:(k + 1) * XCH].rearrange("h w c -> w h c"),
                                           img[s][0:W, k * XCH:(k + 1) * XCH, :]).then_inc(y_st[s][k], 16)
                        if k > 0 and it + 1 < ITERS:
                            pool.wait_ge(y_st[s][k - 1], 16 * (it + 1))
                            load_x(pool, (it + 1) * SUBS + s, s, k - 1, x_ld[s][k - 1])
            for s in range(SUBS):
                for k in range(NXC):
                    pool.wait_ge(y_st[s][k], 16 * ITERS)

        @block.scalar
        def _(act):
            act.wait_ge(ps_clr[0], 1)
            nc.scalar.activation(ps[:, 4:8, :], ps[:, 0:4, :], ACT.Copy).then_inc(ps_clr[1], 1)
            act.wait_ge(ps_clr[1], 1)
            for it, kind, l, s, *what in order:
                m, nb = mid[l], (2, 4)[l]
                if kind == "fwd":
                    if (it, l, s, what[0][0]) == (0, 0, 0, 4):
                        act.wait_ge(grow_clr, 1)
                    for j in what[0]:
                        copy_fwd(act, it, l, s, j, what[1])
                if kind in ("a", "b", "c", "t"):
                    stage_copies(act, "act", kind, act_copy, act_relu, l, mid_count(it, s, what[0]))
                if kind == "d":
                    n, rows = mid_count(it, s, what[0]), (2 * BS, T2 + BS)[l]
                    for q in range(nb):
                        if q >= 2:
                            act.wait_ge(m["d_ss"], n * nb + q - 1)
                        act.wait_ge(m["d_mm"], n * nb + q + 1)
                        act_relu(clip[0:rows, q % 2, :], ps[0:rows, 4 + q, 0:2 * NM]).then_inc(m["d_clip"], 1)
                if kind == "e":
                    if (it, l, s, what[0]) == (0, 0, 0, 0):
                        act.wait_ge(et_clr, 1)
                    n, rows = mid_count(it, s, what[0]), (T2 + 2 * HH, 2 * H)[l]
                    for q in range(nb):
                        act.wait_ge(m["e_mm"], n * nb + q + 1)
                        if n > 0:
                            act.wait_ge(m["e_st"][q], (32, 16)[l] * n)
                        act_copy(et[0:rows, q, 0, :], ps[0:rows, (6, 4)[l] + q, 0:C]).then_inc(m["e_hi"], 1)

        @block.vector
        def _(dve):
            nc.vector.memset(ps[:, 0:4, :], 0.0).then_inc(ps_clr[0], 1)
            for k in range(1, NXC, 2):
                nc.vector.memset(img[0][T2:128, k * XCH:(k + 1) * XCH, :], 0.0).then_inc(img0_clr[1], 1)
                if k == 1:
                    nc.vector.memset(grow[T2:128, :, :], 0.0).then_inc(grow_clr, 1)
            nc.vector.memset(et[4 * KWP:128, :, :, :].bitcast(F32), 0.0).then_inc(et_clr, 1)
            for k in range(NXC):
                nc.vector.memset(img[1][T2:128, k * XCH:(k + 1) * XCH, :], 0.0).then_inc(img1_clr, 1)
            for it, kind, l, s, *what in order:
                m, nb, ph = mid[l], (2, 4)[l], fw_count(it, l, s)
                if kind in ("a", "b", "c", "t"):
                    stage_copies(dve, "dve", kind, dve_copy, dve_relu, l, mid_count(it, s, what[0]))
                if kind == "d":
                    n, rows = mid_count(it, s, what[0]), (2 * BS, T2 + BS)[l]
                    for q in range(nb):
                        dve.wait_ge(m["d_clip"], n * nb + q + 1)
                        for r in range(2):
                            part = slice(r * NM, (r + 1) * NM)
                            dst = ss[0:rows, 2 * q + r, 0:STEPK, 0:H] if l == 0 else ss[0:rows, q, r:2 * STEPK:2, 0:H]
                            last = nc.vector.scalar_tensor_tensor(
                                out=dst, in0=clip[0:rows, q % 2, part].rearrange("p (k m) -> p k m", m=H), scalar=2 * LAM,
                                in1=ps[0:rows, 4 + q, part].rearrange("p (k m) -> p k m", m=H), op0=ALU.min, op1=ALU.subtract)
                        last.then_inc(m["d_ss"], 1)
                if kind == "e":
                    n, rows = mid_count(it, s, what[0]), (T2 + 2 * HH, 2 * H)[l]
                    for q in range(nb):
                        dve.wait_ge(m["e_hi"], n * nb + q + 1)
                        nc.vector.tensor_tensor(et[0:rows, q, 1, :], ps[0:rows, (6, 4)[l] + q, 0:C],
                                                et[0:rows, q, 0, :].bitcast(F32), ALU.subtract).then_inc(m["e_lo"], 1)
                if kind == "inv":
                    for j in what[0]:
                        dve.wait_ge(iw_mm, ph * HP + j + 1)
                        hs = inv_rows(l, j)
                        bank = 4 * what[1] + 2 * (j % 2)
                        if len(hs) == 1:
                            y, p = img[s][0:W, hs[0], :], ps[0:W, bank, 0:C]
                        else:
                            y, p = img[s][0:W, hs[0]:hs[1] + 1:hs[1] - hs[0], :], ps[0:W, bank:bank + 2, 0:C]
                        nc.vector.tensor_tensor(y, p, y, ALU.add).then_inc(iw_add, 1)

        @block.tensor
        def _(pe):
            mm = nc.tensor.matmul
            pe.wait_ge(c_ld, 16)
            for clr in ps_clr:
                pe.wait_ge(clr, 1)

            tenant = [[], [], [], []]

            def wait_all(waits):
                for sem_, n in waits:
                    pe.wait_ge(sem_, n)

            def vacate(pair):
                wait_all(tenant[pair])

            def fwd(l, s, it, jobs, half):
                ph = fw_count(it, l, s)
                for j in jobs:
                    pair = 2 * half + j % 4 // 2
                    if j == jobs[0] or j % 2 == 0:
                        vacate(pair)
                    for k in range(NXC):
                        if l == 0 and 2 * j <= k * XCH < 2 * j + 2:
                            pe.wait_ge(*x_loaded(it, s, k))
                    if l == 1 and j == 0:
                        pe.wait_ge(iw_add, (ph - 1) * HP)
                    for t in range(2):
                        h = 2 * j + t
                        if h < H:
                            last = mm(ps[t * T2:t * T2 + 2 * KWP, 4 * half + j % 4, 0:C], K["w_fwd"], img[s][:, h, :], start=True, stop=True)
                    last.then_inc(fw_mm, 1)
                    tenant[pair] = [(fw_copy, ph * HP + j + 1)]

            def inv(l, s, it, jobs, half):
                ph = fw_count(it, l, s)
                for j in jobs:
                    vacate(2 * half + j % 2)
                    c, at = (j // 2, j % 2) if l == 0 else (j, 0)
                    k = j_ring.slot((it, l, s), c)
                    if at == 0:
                        pe.wait_ge(j_ld[k], j_ring.landed((it, l, s), c))
                    for t, _h in enumerate(inv_rows(l, j)):
                        n = ("w_pos", "w_neg")[t] if l == 0 else "w_one"
                        bank, row = 4 * half + 2 * (j % 2) + t, jslots[k][:, at if l == 0 else t, :]
                        mm(ps[0:W, bank, 0:C], iw_hi[n][:, :], row, start=True, stop=False)
                        last = mm(ps[0:W, bank, 0:C], iw_lo[n][:, :], row, start=False, stop=True)
                    last.then_inc(iw_mm, 1)
                    tenant[2 * half + j % 2] = [(iw_add, ph * HP + j + 1)]

            def stage(kind, l, s, it, i):
                m, nb = mid[l], (2, 4)[l]
                half = nb // 2

                def a_h(n):
                    pe.wait_ge(m["g_ld"], 16 * (n + 1))
                    for q in range(nb):
                        if q % 2 == 0:
                            vacate(q // 2)
                        pair, name = (q, "h_cas") if l == 0 else (q // 2, ("h_re", "h_im")[q % 2])
                        for t in range(2):
                            last = mm(ps[t * T2:t * T2 + H, q, 0:C], K[name], grow[:, 2 * pair + t, :], start=True, stop=True)
                        last.then_inc(m["a_mm"], 1)

                def b_transpose(n):
                    if l == 0:
                        vacate(1)
                    for q in range(nb):
                        pair, b0, bank = (q, 0, 2 + q) if l == 0 else (q // 2, 4 * (q % 2), q)
                        if l == 0:
                            wait_all(copied("a", l, n, [q]))
                        elif q % 2 == 0:
                            wait_all(copied("a", l, n, [q, q + 1]))
                        for b in range(4):
                            last = nc.tensor.transpose(ps[0:2 * BS, bank, b * 128:b * 128 + PR],
                                                       z[0:PR, pair, (b0 + b) * 2 * BS:(b0 + b + 1) * 2 * BS], K["ident"][0:PR, 0:PR])
                        last.then_inc(m["b_mm"], 1)
                    if l == 0:
                        tenant[1] = copied("b", l, n, range(nb))

                def c_block(n):
                    wait_all(copied("b", l, n, range(nb)))
                    for q in range(nb):
                        for b in range(2):
                            last = mm(ps[0:2 * BS, q, b * NM:(b + 1) * NM], w1[l][0:2 * BS + 1, 2 * q + b, :], xt[:, 2 * q + b, :], start=True, stop=True)
                        last.then_inc(m["c_mm"], 1)
                    for k in range(half):
                        tenant[k] = copied("c", l, n, [2 * k, 2 * k + 1])

                def d_block(n):
                    wait_all(copied("c", l, n, range(nb)))
                    for q in range(nb):
                        if q % 2 == 0:
                            vacate(2 + q // 2)
                        for r in range(2):
                            if l == 0:
                                last = mm(ps[0:2 * BS, 4 + q, r * NM:(r + 1) * NM], w2[0][0:2 * BS + 1, 2 * q + r, :], o1[:, 2 * q + r, :], start=True, stop=True)
                            else:
                                for t in range(2):
                                    last = mm(ps[t * T2:t * T2 + BS, 4 + q, r * NM:(r + 1) * NM],
                                              w2[1][0:2 * BS + 1, 2 * q + t, r * BS:(r + 1) * BS], o1[:, 2 * q + t, :], start=True, stop=True)
                        last.then_inc(m["d_mm"], 1)

                def t_transpose(n):
                    pe.wait_ge(m["d_ss"], (n + 1) * nb)
                    if l == 0:
                        vacate(3)
                    for q in range(nb):
                        rows, wide, bank = (2 * BS, 2 * BS, 6 + q) if l == 0 else (T2 + BS, 128, 4 + q)
                        for b in range(4):
                            modes = ss[0:rows, b, 2 * q:2 * q + 2, :].rearrange("p k m -> p (k m)")[:, 0:PR]
                            last = nc.tensor.transpose(ps[0:PR, bank, b * wide:b * wide + rows], modes, K["ident"][0:rows, 0:rows])
                        last.then_inc(m["t_mm"], 1)

                def e_h(n):
                    for q in range(nb):
                        wait_all(copied("t", l, n, [q]))
                        if l == 0:
                            for t in range(2):
                                last = mm(ps[t * T2:t * T2 + 2 * HH, 6 + q, 0:C], K[("u0_lo", "u0_hi")[t]][0:PR, :],
                                          spec[0:PR, q, :], start=True, stop=True)
                        else:
                            last = mm(ps[0:2 * H, 4 + q, 0:C], K["u1"][0:PR, :], spec[0:PR, q, :], start=True, stop=True)
                        last.then_inc(m["e_mm"], 1)
                    for k in range(half):
                        tenant[3 if l == 0 else 2 + k] = [(m["e_lo"], n * nb + 2 * k + 2)]

                {"a": a_h, "b": b_transpose, "c": c_block, "d": d_block, "t": t_transpose, "e": e_h}[kind](mid_count(it, s, i))

            for it, kind, l, s, *what in order:
                if kind == "fwd":
                    fwd(l, s, it, *what)
                elif kind == "inv":
                    if (it, l, s, what[0][0]) == (0, 0, 0, 0):
                        pe.wait_ge(wfix, 6)
                        pe.wait_ge(iw_ok, 6)
                    inv(l, s, it, *what)
                elif kind in "abcdte":
                    if (it, kind, s, *what) == (0, "c", 0, 0):
                        pe.wait_ge(wfix, (5, 8)[l])
                        pe.wait_ge(w_ld[l], 16 * (6, 12)[l])
                        pe.wait_ge(w_ok[l], (1, 3)[l])
                    stage(kind, l, s, it, *what)
            pe.wait_ge(iw_add, (fw_count(it, 1, 1) + 1) * HP)
    return nc


def kernel(**inputs):
    import concourse.bacc as bacc
    from concourse.bass_utils import run_bass_kernel_spmd

    nc = bacc.Bacc("TRN2", target_bir_lowering=False, num_devices=1)
    const, where = constants()
    arrays, args = {}, []
    names = ["x"] + [f"L{l}_conv_{n}" for l in range(2) for n in ("w1", "b1", "w2", "b2")]
    for name in names:
        arrays[name] = np.ascontiguousarray(inputs[name])
    arrays["const"] = const
    for name, a in arrays.items():
        args.append(nc.dram_tensor(name, a.shape, mybir.dt.from_np(a.dtype), kind="ExternalInput").ap())
    out = nc.dram_tensor("y", (B, H, W, C), F32, kind="ExternalOutput").ap()
    spectral_layers(nc, *args, out, where)
    r = run_bass_kernel_spmd(nc, [arrays], core_ids=[0])
    return r.results[0]["y"]
```
